# Optimizing a Trainium2 kernel written in Bass

```python
import numpy as np
import jax
import jax.numpy as jnp

def _softmax(x, axis=-1):
    return jax.nn.softmax(x, axis=axis)
def _gelu(x):
    return jax.nn.gelu(x, approximate=True)
def _silu(x):
    return jax.nn.silu(x)
def _sigmoid(x):
    return jax.nn.sigmoid(x)
def _layernorm(x, axis=-1, eps=1e-5):
    m = jnp.mean(x, axis=axis, keepdims=True)
    v = jnp.var(x, axis=axis, keepdims=True)
    return (x - m) / jnp.sqrt(v + eps)
def _scatter_add(tgt, idx, src, axis=0):
    return tgt.at[idx].add(src)
def _segment_sum(src, seg, n):
    return jax.ops.segment_sum(src, seg, n)

kernel_name = 'mk_adj_preln_d2_adj_512_eabbc8'

def setup_inputs(seed: int = 0):
    np.random.seed(seed)
    _w = jnp.asarray
    def _rec_inputs():
        import jax
        import jax.numpy as jnp
        _gk = jax.random.key(seed)
        x = -0.0005207 + 1.001 * jax.random.normal(jax.random.fold_in(_gk, 1), (3327, 512), jnp.float32)
        _a = jax.random.bernoulli(jax.random.fold_in(_gk, 2), 0.00240457, (3327, 3327))
        adj = _a.astype(jnp.int32)
        return x, adj
    x, adj = _rec_inputs()
    def _L0_gnn_setup():
        import jax, jax.numpy as jnp
        import numpy as np
        ALPHA = 0.2
        NEG_INF = -9000000000000000.0
        N, IN_F, H, OUT_F = (4096, 512, 4, 128)
        key = jax.random.key(seed)
        ks = jax.random.split(key, 6)
        x = jax.random.normal(ks[0], (N, IN_F), dtype=jnp.float32)
        adj = jax.random.randint(ks[1], (N, N), 0, 2, dtype=jnp.int32)
        M = jax.random.uniform(ks[2], (N, N), dtype=jnp.float32)
        W = jax.random.normal(ks[3], (IN_F, H * OUT_F), dtype=jnp.float32) * (1.414 * (2.0 / (IN_F + H * OUT_F)) ** 0.5)
        a_self = jax.random.normal(ks[4], (1, H, OUT_F), dtype=jnp.float32) * 0.1
        a_neighs = jax.random.normal(ks[5], (1, H, OUT_F), dtype=jnp.float32) * 0.1
        return {'x': x, 'adj': adj, 'M': M, 'W': W, 'a_self': a_self, 'a_neighs': a_neighs}
    _L0_gnn_all = _L0_gnn_setup()
    _L0_gnn_in = {k: v for k, v in _L0_gnn_all.items() if k in ('W', 'a_self', 'a_neighs', )}
    del _L0_gnn_all

    def _L1_gnn_setup():
        import jax, jax.numpy as jnp
        import numpy as np
        key = jax.random.key(seed)
        kX, kA, k1, k2, k3, k4 = jax.random.split(key, 6)
        N, Cin, Cout = (8192, 512, 512)
        X = jax.random.normal(kX, (N, Cin), dtype=jnp.float32)
        A = jax.random.randint(kA, (N, N), 0, 2, dtype=jnp.int32)
        bound = 1.0 / np.sqrt(Cin)
        W_nb = jax.random.uniform(k1, (Cout, Cin), jnp.float32, -bound, bound)
        b_nb = jax.random.uniform(k2, (Cout,), jnp.float32, -bound, bound)
        W_line = jax.random.uniform(k3, (Cout, Cin), jnp.float32, -bound, bound)
        b_line = jax.random.uniform(k4, (Cout,), jnp.float32, -bound, bound)
        return {'X': X, 'A': A, 'W_nb': W_nb, 'b_nb': b_nb, 'W_line': W_line, 'b_line': b_line, 'neibor_num': 64}
    _L1_gnn_all = _L1_gnn_setup()
    _L1_gnn_in = {k: v for k, v in _L1_gnn_all.items() if k in ('W_nb', 'b_nb', 'W_line', 'b_line', )}
    del _L1_gnn_all

    return {
        "x": x,
        "adj": adj,
        "L0_gnn_W": _L0_gnn_in["W"],
        "L0_gnn_a_self": _L0_gnn_in["a_self"],
        "L0_gnn_a_neighs": _L0_gnn_in["a_neighs"],
        "L1_gnn_W_nb": _L1_gnn_in["W_nb"],
        "L1_gnn_b_nb": _L1_gnn_in["b_nb"],
        "L1_gnn_W_line": _L1_gnn_in["W_line"],
        "L1_gnn_b_line": _L1_gnn_in["b_line"],
    }

def reference(x, adj, L0_gnn_W, L0_gnn_a_self, L0_gnn_a_neighs, L1_gnn_W_nb, L1_gnn_b_nb, L1_gnn_W_line, L1_gnn_b_line):
    import jax
    import jax.numpy as jnp
    def _L0_gnn_ref(x, adj, M, W, a_self, a_neighs):
        import jax, jax.numpy as jnp
        import numpy as np
        ALPHA = 0.2
        NEG_INF = -9000000000000000.0
        N, IN_F, H, OUT_F = (4096, 512, 4, 128)
        h = (x @ W).reshape(-1, H, OUT_F)
        attn_s = jnp.sum(h * a_self, axis=-1)
        attn_n = jnp.sum(h * a_neighs, axis=-1)
        scores = attn_s.T[:, :, None] + attn_n.T[:, None, :]
        scores = scores * M[None, :, :]
        scores = jnp.where(scores >= 0, scores, ALPHA * scores)
        scores = jnp.where(adj[None, :, :] > 0, scores, NEG_INF)
        attention = jax.nn.softmax(scores, axis=-1)
        h_prime = jnp.einsum('hij,jhf->ihf', attention, h)
        return h_prime.reshape(-1, H * OUT_F)

    def _L1_gnn_ref(X, A, W_nb, b_nb, W_line, b_line, neibor_num):
        import jax, jax.numpy as jnp
        import numpy as np
        Ab = A > 0
        keep = Ab & (jnp.cumsum(Ab.astype(jnp.int32), axis=1) <= neibor_num)
        cnt = keep.sum(axis=1, keepdims=True).astype(X.dtype)
        nb_sum = keep.astype(X.dtype) @ X
        nb_mean = nb_sum / jnp.maximum(cnt, 1.0)
        xj = jax.nn.leaky_relu(nb_mean @ W_nb.T + b_nb)
        xi = jax.nn.leaky_relu(X @ W_line.T + b_line)
        return xi + jnp.where(cnt > 0, xj, jnp.zeros((), X.dtype))

    h = jnp.maximum(_layernorm(x, axis=-1), 0.0)
    x = x + _L0_gnn_ref(h, adj, adj, L0_gnn_W, L0_gnn_a_self, L0_gnn_a_neighs)
    h = jnp.maximum(_layernorm(x, axis=-1), 0.0)
    x = x + _L1_gnn_ref(h, adj, L1_gnn_W_nb, L1_gnn_b_nb, L1_gnn_W_line, L1_gnn_b_line, 64)
    return x


_drawn_inputs = setup_inputs


def setup_inputs(seed=0):
    import zlib

    import numpy as np

    out = dict(_drawn_inputs(seed))
    spreads = {}
    factors = {'L1_gnn_b_nb': 4.181, 'L1_gnn_b_line': 3.827}
    for name, (base, spread) in spreads.items():
        noise = np.random.default_rng([zlib.crc32(name.encode()), seed]).standard_normal(out[name].shape)
        drawn = base * np.exp(spread * noise) if base else spread * noise
        out[name] = jnp.asarray(drawn.astype(out[name].dtype))
    for name, factor in factors.items():
        out[name] = (out[name] * factor).astype(out[name].dtype)
    return out
```

```python
from contextlib import ExitStack

import concourse.bass as bass
from concourse import mybir

F32 = mybir.dt.float32
F16 = mybir.dt.float16
BF16 = mybir.dt.bfloat16
I32 = mybir.dt.int32
U8 = mybir.dt.uint8
ALU = mybir.AluOpType
ACT = mybir.ActivationFunctionType
AX_X = mybir.AxisListType.X
ds = bass.ds


def gnn_two_layers(nc, x, adj, W, a_self, a_neighs, W_nb, b_nb, W_line, b_line, out):
    N, C = x.shape
    P = 128
    NT = -(-N // P)
    NP = NT * P
    LAST = N - (NT - 1) * P
    KT = C // P
    H, FH = a_self.shape[1], a_self.shape[2]
    FA = FH + 1
    CHUNKS = 2
    CT = NT // CHUNKS
    CW = CT * P
    NEIGH = 64
    ALPHA = 0.2
    SLOPE = 0.01
    EPS = 1e-5
    YS = 128.0
    U_TOP = 100.0
    HALVES = 16
    G = [7, 7, 6, 6]
    GO = [sum(G[:g]) for g in range(len(G))]
    NG = len(G)
    assert sum(G) == NT and NT % 2 == 0 and CT * CHUNKS == NT and H * FH == C == 512
    ROWS = [(0, LAST // 16 * 16), (LAST // 16 * 16, LAST)] if LAST % 16 else [(0, LAST)]
    NR = len(ROWS)

    r_dram = nc.dram_tensor("r_rows", [H * NT, P], F32, kind="Internal").ap()
    r_flat = r_dram.rearrange("(a t) p -> a (t p)", a=1)
    z_dram = nc.dram_tensor("z_rows", [NP, C], F32, kind="Internal").ap()

    with ExitStack() as ctx:
        def sb(name, shape, dt):
            return ctx.enter_context(nc.sbuf_tensor(name, shape, dt))

        def sem(name):
            return ctx.enter_context(nc.semaphore(name))

        adjT = sb("adjT", [P, NT, NP], U8)
        slots = sb("slots", [P, H + 1, NT, FA], F32)
        work = sb("work", [P, 6 * CW], F32)
        aux = sb("aux", [P, 6, C], F32)
        adj_i = work[:, 0:2 * NP].bitcast(I32).rearrange("p (s n) -> p s n", s=2)
        adj_b = work[:, 2 * NP:3 * NP].bitcast(BF16).rearrange("p (s n) -> p s n", s=2)
        R = work[:, 0:2 * CW].rearrange("p (s n) -> p s n", s=2)
        q = work[:, 2 * CW:4 * CW].rearrange("p (s n) -> p s n", s=2)
        Pt = work[:, 4 * CW:6 * CW].rearrange("p (s n) -> p s n", s=2)
        wT = work[:, 0:2 * KT * C].rearrange("p (w k n) -> p w k n", w=2, k=KT)
        x1 = work[:, 2 * KT * C:2 * KT * C + 2 * C].rearrange("p (s n) -> p s n", s=2)
        xo = work[:, 2 * KT * C + 2 * C:2 * KT * C + 4 * C].rearrange("p (s n) -> p s n", s=2)
        zt = work[:, 2 * KT * C + 4 * C:2 * KT * C + 6 * C].rearrange("p (s n) -> p s n", s=2)
        zl = work[:, 2 * KT * C + 6 * C:2 * KT * C + 8 * C].rearrange("p (s n) -> p s n", s=2)
        zo = work[:, 2 * KT * C + 8 * C:2 * KT * C + 10 * C].rearrange("p (s n) -> p s n", s=2)
        bline = work[:, 2 * KT * C + 10 * C:2 * KT * C + 11 * C]
        keep16 = work[:, 0:NP].bitcast(F16).rearrange("p (s j i) -> p s j i", s=2, j=NT)
        zin = work[:, NP:NP + 2 * C].rearrange("p (s n) -> p s n", s=2)
        dt_ = work[:, NP + 2 * C:NP + 4 * C].rearrange("p (s n) -> p s n", s=2)
        dl = work[:, NP + 4 * C:NP + 6 * C].rearrange("p (s n) -> p s n", s=2)
        do = work[:, NP + 6 * C:NP + 8 * C].rearrange("p (s n) -> p s n", s=2)
        bnb = work[:, NP + 8 * C:NP + 9 * C]
        xb, hn, hT = (aux[:, 2 * k:2 * k + 2, :] for k in range(3))
        w_nb_raw = aux[:, 2:6, :]
        flat_slots = slots[:, :, :, :].rearrange("p s t f -> p s (t f)")
        W0 = flat_slots[:, 0, 0:KT * C].rearrange("p (k n) -> p k n", k=KT)
        a_bc = flat_slots[:, 0, KT * C:KT * C + 2 * C].rearrange("p (a n) -> p a n", a=2)
        w_line_raw = flat_slots[:, H, 0:KT * C].rearrange("p (k n) -> p k n", k=KT)
        count = flat_slots[:, H, KT * C:KT * C + NP // 4 + 1].bitcast(U8)
        y16 = slots[:, :, :, 0:FH].bitcast(F16).rearrange("p s t (a f) -> p s t a f", a=2)
        hmean = sb("hmean", [P, C], F32)
        hsum = a_bc[:, 0, :]
        rT = q[0:H * NT, 0, 0:P]
        hsumT = q[:, 1, 0:KT * P].rearrange("p (k n) -> p k n", k=KT)
        wa = sb("wa", [P, KT, 2 * H], F32)
        ident = sb("ident", [P, P], F32)
        ident_b = sb("ident_b", [P, P], BF16)
        ones = sb("ones", [P, P], F32)
        eps = sb("eps", [P, 1], F32)
        cap = sb("cap", [P, 1], F32)
        stats = sb("stats", [P, 2, 6], F32)
        both = sb("both", [P, 2, 2], F32)
        gap = sb("gap", [P, 2, 2], F32)
        cvar = sb("cvar", [P, 2], F32)
        std = sb("std", [P, 2], F32)
        rstd = sb("rstd", [P, 2], F32)
        nbias = sb("nbias", [P, 2], F32)
        sn = sb("sn", [P, 2 * H, NT], F32)
        cnt = sb("cnt", [P, NT], F32)
        top = sb("top", [P, H + 1], F32)
        topa = sb("topa", [P, H + 1], F32)
        Fj = sb("Fj", [P, H, NT], F32)
        r_i = sb("r_i", [P, H, NT], F32)
        Kj = sb("Kj", [P, H, NT], F32)
        nKj = sb("nKj", [P, H, NT], F32)
        flag = sb("flag", [P, 1], I32)
        empty = sb("empty", [P, NT], F32)
        some = sb("some", [P, NT], F32)
        rcnt = sb("rcnt", [P, NT], F32)
        den = sb("den", [P, CT], F32)
        ps = ctx.enter_context(nc.psum_tensor("ps", [P, 8, C], F32))
        psb = ps[:, :, :].bitcast(BF16)
        TPB = 3
        NB = -(-CT // TPB)

        def acc(m):
            return ps[:, m // TPB, (m % TPB) * FA:(m % TPB + 1) * FA]

        s_x = [sem(f"x_loaded{s}") for s in range(2)]
        s_adj = [sem(f"adj_loaded{s}") for s in range(2)]
        s_w0 = sem("w0_loaded")
        s_av = sem("a_loaded")
        s_const = sem("consts_set")
        s_pad = sem("pad_rows_zeroed")
        s_bn = sem("bn_stats_done")
        s_gap = sem("mean_gap_done")
        s_gap2 = sem("mean_gap_squared")
        s_mv = sem("variance_done")
        s_std = sem("std_done")
        s_rstd = sem("rstd_done")
        s_coef = sem("ln_coefs_done")
        s_hn = sem("hn_done")
        s_hs0 = sem("hsum_zeroed")
        s_hsum = sem("hsum_added")
        s_wap = sem("wa_product_done")
        s_wa = sem("wa_done")
        s_cast = sem("adj_cast_done")
        s_xT = sem("x_transposed")
        s_hT = sem("hT_copied")
        s_mm = sem("h_product_done")
        s_hev = sem("h_copied")
        s_g = sem("adj_group_transposed")
        s_gev = sem("adj_group_copied")
        s_top = sem("tops_done")
        s_topa = sem("tops_all_done")
        s_nd = sem("shifted_scores_done")
        s_nd1 = sem("u_added")
        s_exp = sem("exps_done")
        s_nk = sem("minus_k_done")
        s_rt = sem("r_transposed")
        s_rtc = sem("rT_copied")
        s_rout = sem("r_stored")
        s_R = [sem(f"R_loaded{c}") for c in range(CHUNKS)]
        s_flag = sem("flag_done")
        s_cn0 = sem("count_steps_done")
        s_hst = sem("hsum_transposed")
        s_hstc = sem("hsumT_copied")
        s_hm = sem("hmean_product_done")
        s_hmc = sem("hmean_done")
        s_q = sem("q_ready")
        s_p = sem("p_ready")
        s_pe = sem("p_consumed")
        s_den = sem("den_done")
        s_rden = sem("rden_done")
        s_ev = sem("bank_copied")
        c_adj = [sem(f"c1_adj_loaded{s}") for s in range(2)]
        c_pad = sem("c1_pad_zeroed")
        c_zero = sem("c1_zeros_set")
        c_scan = sem("c1_scan_done")
        c_dif = sem("c1_keep_done")
        c_g = sem("c1_group_transposed")
        c_gev = sem("c1_group_copied")
        s_wnb = sem("w_nb_loaded")
        s_wl = sem("w_line_loaded")
        s_bl = sem("b_line_loaded")
        s_bnb = sem("b_nb_loaded")
        s_wt = sem("w_transposed")
        s_wtc = [sem("w_nbT_copied"), sem("w_lineT_copied")]
        s_x2 = [sem(f"x_again_loaded{s}") for s in range(2)]
        s_xo = sem("xo_done")
        s_x1 = sem("x1_done")
        s_z = sem("z_product_done")
        s_yz = sem("y_product_done")
        s_yhi = sem("y_hi_done")
        s_ylo = sem("y_lo_done")
        s_zt = sem("z_biased")
        s_zl = sem("z_leaky")
        s_zo = sem("z_done")
        s_zs = [sem(f"z_stored{s}") for s in range(2)]
        s_k16 = sem("keep16_done")
        s_nb = sem("neighbour_sums_done")
        s_dt = sem("mean_biased")
        s_dl = sem("mean_leaky")
        s_do = sem("out_tile_done")
        s_zin = [sem(f"z_loaded{s}") for s in range(2)]
        s_out = [sem(f"out_stored{s}") for s in range(2)]

        LN_A = NT
        X_A = [HALVES * NT // 2, HALVES * (NT // 2 - 1 + NR)]
        GROUPS = NG * NT
        STEPS = H * CHUNKS * NT

        def in_pairs(eng, body, start=0):
            for s in range(2):
                body(s, s, s == 0, False)
            with eng.Fori(1, NT // 2 - 1) as i:
                for s in range(2):
                    body(i * 2 + s, s, False, False)
            for s in range(2):
                body(NT - 2 + s, s, False, s == 1)

        block = ctx.enter_context(nc.Block())

        @block.sync
        def _(sp):
            def load_rows(dst, src, t, s, semaphore, last, cols=None):
                if not last:
                    sp.dma_start(dst[:, s, 0:src.shape[1]], src[ds(t * P, P), :]).then_inc(semaphore, HALVES)
                else:
                    for a, b in ROWS:
                        sp.dma_start(dst[a:b, s, 0:src.shape[1]], src[(NT - 1) * P + a:(NT - 1) * P + b, :]) \
                          .then_inc(semaphore, HALVES)

            def stage_a(t, s, first, last):
                static = isinstance(t, int)
                if not (static and t < 2):
                    sp.wait_ge(s_hn, t - 1)
                if last:
                    sp.wait_ge(s_pad, 1)
                load_rows(xb, x, t, s, s_x[s], last)
                if not (static and t < 2):
                    sp.wait_ge(s_cast, t - 1)
                if last:
                    sp.wait_ge(s_pad, 2)
                load_rows(adj_i, adj, t, s, s_adj[s], last)
                if static and t == 0:
                    sp.dma_start(W0, W.rearrange("(k p) n -> p k n", p=P)).then_inc(s_w0, HALVES)
                    for k, a in enumerate((a_self, a_neighs)):
                        sp.dma_start(a_bc[:, k, :], a.rearrange("a h f -> a (h f)").to_broadcast([P, C])) \
                          .then_inc(s_av, HALVES)

            in_pairs(sp, stage_a)

            sp.wait_ge(s_rtc, 1)
            sp.dma_start(r_dram, rT).then_inc(s_rout, HALVES)
            sp.wait_ge(s_rout, HALVES)
            sp.wait_ge(s_cast, NT)
            for c in range(CHUNKS):
                sp.dma_start(R[:, c, :], r_flat[:, c * CW:(c + 1) * CW].to_broadcast([P, CW])) \
                  .then_inc(s_R[c], HALVES)
            with sp.Fori(1, H) as h:
                for c in range(CHUNKS):
                    sp.wait_ge(s_q, (h * CHUNKS + (c - 1)) * NT)
                    sp.dma_start(R[:, c, :], r_flat[:, ds(h * NP + c * CW, CW)].to_broadcast([P, CW])) \
                      .then_inc(s_R[c], HALVES)
            sp.wait_ge(s_hmc, 1)
            sp.wait_ge(s_mm, NT)
            sp.wait_ge(s_hsum, NT)
            sp.dma_start(w_nb_raw, W_nb.rearrange("(k p) n -> p k n", p=P)).then_inc(s_wnb, HALVES)
            sp.dma_start(xb[:, 0, :], x[0:P, :]).then_inc(s_x2[0], HALVES)
            sp.dma_start(xb[:, 1, :], x[P:2 * P, :]).then_inc(s_x2[1], HALVES)
            sp.wait_ge(s_pe, STEPS)
            sp.dma_start(w_line_raw, W_line.rearrange("(k p) n -> p k n", p=P)).then_inc(s_wl, HALVES)

            sp.wait_ge(s_flag, 1)
            many = sp.value_load(flag[0:1, 0:1], min_val=0, max_val=1)
            with sp.If(many > 0):
                def c1(t, s, first, last):
                    if not (isinstance(t, int) and t < 2):
                        sp.wait_ge(c_scan, t - 1)
                    if last:
                        sp.wait_ge(c_pad, 1)
                    load_rows(adj_i, adj, t, s, c_adj[s], last)
                in_pairs(sp, c1)
                sp.wait_ge(c_gev, GROUPS)

            sp.wait_ge(s_ev, H * CHUNKS * NB)
            sp.wait_ge(s_pe, STEPS)
            sp.dma_start(bline, b_line.rearrange("(a n) -> a n", a=1).to_broadcast([P, C])).then_inc(s_bl, HALVES)

            def stage_c2(t, s, first, last):
                if not first and not last:
                    sp.wait_ge(s_xo, t)
                    load_rows(xb, x, t + 1, 1 - s, s_x2[1 - s], isinstance(t, int) and t + 1 == NT - 1)
                if not (isinstance(t, int) and t < 1):
                    store_z(t - 1, 1 - s)

            def store_z(t, s):
                sp.wait_ge(s_zo, t + 1)
                sp.dma_start(z_dram[ds(t * P, P), :], zo[:, s, :]).then_inc(s_zs[s], HALVES)

            in_pairs(sp, stage_c2)
            store_z(NT - 1, 1)

            sp.wait_ge(s_zt, NT)
            sp.wait_ge(s_yz, NT)
            for s in range(2):
                sp.wait_ge(s_zs[s], HALVES * NT // 2)
            sp.dma_start(bnb, b_nb.rearrange("(a n) -> a n", a=1).to_broadcast([P, C])).then_inc(s_bnb, HALVES)

            def stage_d(t, s, first, last):
                if not (isinstance(t, int) and t < 2):
                    sp.wait_ge(s_do, t - 1)
                sp.dma_start(zin[:, s, :], z_dram[ds(t * P, P), :]).then_inc(s_zin[s], HALVES)
                if not (isinstance(t, int) and t < 1):
                    store_out(t - 1, 1 - s)

            def store_out(t, s):
                sp.wait_ge(s_do, t + 1)
                sp.dma_start(out[ds(t * P, P), :], do[:, s, :]).then_inc(s_out[s], HALVES)

            in_pairs(sp, stage_d)
            sp.wait_ge(s_do, NT)
            for a, b in ROWS:
                sp.dma_start(out[(NT - 1) * P + a:(NT - 1) * P + b, :], do[a:b, 1, :]).then_inc(s_out[1], HALVES)
            sp.wait_ge(s_out[0], HALVES * NT // 2)
            sp.wait_ge(s_out[1], HALVES * (NT // 2 - 1 + NR))

        @block.gpsimd
        def _(pool):
            nc.gpsimd.memset(ident[:, :], 0.0).then_inc(s_const, 1)
            nc.gpsimd.memset(ones[:, :], 1.0).then_inc(s_const, 1)
            nc.gpsimd.memset(eps[:, :], EPS).then_inc(s_const, 1)
            nc.gpsimd.memset(cap[:, :], float(NEIGH)).then_inc(s_const, 1)
            nc.gpsimd.memset(adj_b[:, :, N:NP], 0.0).then_inc(s_const, 1)
            pool.wait_ge(s_const, 5)
            nc.gpsimd.affine_select(out=ident[:, :], in_=ident[:, :], compare_op=ALU.not_equal, fill=1.0, base=0,
                                    pattern=[[-1, P]], channel_multiplier=1).then_inc(s_const, 1)
            pool.wait_ge(s_const, 6)
            nc.gpsimd.tensor_copy(ident_b[:, :], ident[:, :]).then_inc(s_const, 1)
            nc.gpsimd.memset(slots[:, 1:H + 1, :, FH:FA], 1.0).then_inc(s_const, 1)

            pool.wait_ge(s_wa, 2 * KT)
            nc.gpsimd.memset(hsum, 0.0).then_inc(s_hs0, 1)
            pool.wait_ge(s_hs0, 1)

            def sum_h(t, s, first, last):
                pool.wait_ge(s_hn, t + 1)
                if not first:
                    pool.wait_ge(s_hsum, t)
                nc.gpsimd.tensor_tensor(hsum, hsum, hn[:, s, :], ALU.add).then_inc(s_hsum, 1)
                if isinstance(t, int) and t == NT - 3:
                    pool.wait_ge(s_hsum, NT - 2)
                    nc.gpsimd.memset(xb[P - 32:P, 1, :], 0.0).then_inc(s_pad, 1)
                    pool.wait_ge(s_cast, NT - 2)
                    pool.wait_ge(s_pad, 1)
                    nc.gpsimd.memset(adj_i[P - 32:P, 1, :], 0).then_inc(s_pad, 1)
                    pool.wait_ge(s_pad, 2)

            for s in range(2):
                sum_h(s, s, s == 0, False)
            with pool.Fori(1, NT // 2 - 2) as i:
                for s in range(2):
                    sum_h(i * 2 + s, s, False, False)
            for t in range(NT - 4, NT):
                sum_h(t, t % 2, False, t == NT - 1)

            pool.wait_ge(s_top, 2)
            nc.gpsimd.partition_all_reduce(topa[:, :], top[:, :], P, bass.bass_isa.ReduceOp.max).then_inc(s_topa, 1)

            pool.wait_ge(s_flag, 1)
            many = pool.value_load(flag[0:1, 0:1], min_val=0, max_val=1)
            with pool.If(many > 0):
                pool.wait_ge(c_scan, NT - 2)
                nc.gpsimd.memset(adj_i[P - 32:P, 1, :], 0).then_inc(c_pad, 1)
                pool.wait_ge(c_pad, 1)

            pool.wait_ge(s_ev, H * CHUNKS * NB)
            pool.wait_ge(s_pe, STEPS)

            def add_x(t, s, last):
                if not (isinstance(t, int) and t < 2):
                    pool.wait_ge(s_x1, t - 1)
                if last:
                    pool.wait_ge(s_x2[s], HALVES * (NT // 2 - 1 + NR))
                elif isinstance(t, int):
                    pool.wait_ge(s_x2[s], HALVES * (t // 2 + 1))
                else:
                    pool.wait_ge(s_x2[s], (t - s) * (HALVES // 2) + HALVES)
                nc.gpsimd.tensor_tensor(xo[:, s, :].rearrange("p (h f) -> p h f", h=H),
                                        xb[:, s, :].rearrange("p (h f) -> p h f", h=H),
                                        slots[:, 0:H, ds(t, 1), 0:FH].rearrange("p h a f -> p h (a f)"),
                                        ALU.add).then_inc(s_xo, 1)

            def add_z(t, s):
                pool.wait_ge(s_zl, t + 1)
                if not (isinstance(t, int) and t < 2):
                    if isinstance(t, int):
                        pool.wait_ge(s_zs[s], HALVES * (t // 2))
                    else:
                        pool.wait_ge(s_zs[s], (t - s) * (HALVES // 2))
                nc.gpsimd.tensor_tensor(zo[:, s, :], zl[:, s, :], x1[:, s, :], ALU.add).then_inc(s_zo, 1)

            def stage_c2(t, s, first, last):
                if not last:
                    add_x(t + 1, 1 - s, isinstance(t, int) and t + 1 == NT - 1)
                if not first:
                    add_z(t - 1, 1 - s)

            add_x(0, 0, False)
            in_pairs(pool, stage_c2)
            add_z(NT - 1, 1)

        @block.scalar
        def _(act):
            def std_relu(t, s, base, src, semaphores):
                act.wait_ge(s_mv, base + t + 1)
                nc.scalar.activation(std[:, s:s + 1], cvar[:, s:s + 1], ACT.Sqrt, bias=eps[:, 0:1],
                                     scale=1.0 / C).then_inc(s_std, 1)
                act.wait_ge(s_coef, base + t + 1)
                for sm, v in semaphores:
                    act.wait_ge(sm, v)
                nc.scalar.activation(hn[:, s, :], src[:, s, :], ACT.Relu, bias=nbias[:, s:s + 1],
                                     scale=rstd[:, s:s + 1]).then_inc(s_hn, 1)

            def cast(t, s, last):
                if last:
                    act.wait_ge(s_adj[s], X_A[1])
                elif isinstance(t, int):
                    act.wait_ge(s_adj[s], HALVES * (t // 2 + 1))
                else:
                    act.wait_ge(s_adj[s], (t - s) * (HALVES // 2) + HALVES)
                if not (isinstance(t, int) and t < 2):
                    act.wait_ge(s_g, NG * (t - 1))
                nc.scalar.activation(adj_b[:, s, 0:N], adj_i[:, s, 0:N], ACT.Copy,
                                     accum_out=cnt[:, ds(t, 1)]).then_inc(s_cast, 1)

            def copy_hT(t, s, base):
                act.wait_ge(s_xT, base + t + 1)
                if not (isinstance(t, int) and t < 2):
                    act.wait_ge(s_mm if base == 0 else s_yz, t - 1)
                nc.scalar.activation(hT[:, s, :], ps[:, s, :], ACT.Copy).then_inc(s_hT, 1)

            def copy_h(t, s):
                act.wait_ge(s_mm, t + 1)
                nc.scalar.activation(slots[:, 1:H + 1, ds(t, 1), 0:FH].rearrange("p h a f -> p h (a f)"),
                                     ps[:, 2 + s, :].rearrange("p (h f) -> p h f", h=H), ACT.Copy)
                nc.scalar.activation(sn[:, :, ds(t, 1)].rearrange("p h a -> p (h a)"), ps[:, 4 + s, 0:2 * H],
                                     ACT.Copy).then_inc(s_hev, 1)

            def a_waits(t):
                if isinstance(t, int) and t < 2:
                    return []
                return [(s_xT, t - 1), (s_hsum, t - 1)]

            def stage_a(t, s, first, last):
                if not last:
                    std_relu(t + 1, 1 - s, 0, xb, a_waits(t + 1))
                copy_hT(t, s, 0)
                if not last:
                    cast(t + 1, 1 - s, isinstance(t, int) and t + 1 == NT - 1)
                if not first:
                    copy_h(t - 1, 1 - s)

            act.wait_ge(s_const, 8)
            std_relu(0, 0, 0, xb, [])
            cast(0, 0, False)
            in_pairs(act, stage_a)
            copy_h(NT - 1, 1)

            act.wait_ge(s_nd, 2)
            nc.scalar.activation(r_i[:, :, :], r_i[:, :, :], ACT.Exp, scale=1.0 - ALPHA).then_inc(s_exp, 1)
            nc.scalar.activation(Kj[:, :, :], Fj[:, :, :], ACT.Exp, scale=ALPHA).then_inc(s_exp, 1)
            nc.scalar.activation(Fj[:, :, :], Fj[:, :, :], ACT.Exp).then_inc(s_exp, 1)
            act.wait_ge(s_rt, 1)
            nc.scalar.activation(rT, ps[0:H * NT, 0, 0:P], ACT.Copy).then_inc(s_rtc, 1)
            act.wait_ge(s_hst, 1)
            nc.scalar.activation(hsumT, ps[:, 1, :].rearrange("p (k n) -> p k n", k=KT),
                                 ACT.Copy).then_inc(s_hstc, 1)
            act.wait_ge(s_hm, 1)
            nc.scalar.activation(hmean[:, :], ps[:, 2, :], ACT.Copy, scale=1.0 / N).then_inc(s_hmc, 1)

            act.wait_ge(s_nk, 1)
            act.wait_ge(s_exp, 3)
            act.wait_ge(s_gev, GROUPS)
            act.wait_ge(s_g, GROUPS)

            def q_step(h, c, j, s, first):
                step = (h * CHUNKS + c) * NT + j
                if not first:
                    act.wait_ge(s_p, step - 1)
                nc.scalar.activation(q[:, s, :], R[:, c, :], ACT.Relu, bias=nKj[:, ds(h, 1), ds(j, 1)].rearrange("p a b -> p (a b)"),
                                     scale=Fj[:, ds(h, 1), ds(j, 1)].rearrange("p a b -> p (a b)")).then_inc(s_q, 1)

            for c in range(CHUNKS):
                act.wait_ge(s_R[c], HALVES)
                for j in range(2):
                    q_step(0, c, j, j, c == 0)
                with act.Fori(1, NT // 2) as i:
                    for s in range(2):
                        q_step(0, c, i * 2 + s, s, False)
            with act.Fori(1, H) as h:
                for c in range(CHUNKS):
                    act.wait_ge(s_R[c], h * HALVES + HALVES)
                    with act.Fori(0, NT // 2) as i:
                        for s in range(2):
                            q_step(h, c, i * 2 + s, s, False)

            act.wait_ge(s_pe, STEPS)
            act.wait_ge(s_ev, H * CHUNKS * NB)
            act.wait_ge(s_flag, 1)
            many = act.value_load(flag[0:1, 0:1], min_val=0, max_val=1)
            with act.If(many > 0):
                act.wait_ge(c_gev, GROUPS)
            for k in range(KT):
                act.wait_ge(s_wt, 2 * k + 1)
                nc.scalar.activation(wT[:, 0, k, :], ps[:, 2 * (k % 2), :], ACT.Copy).then_inc(s_wtc[0], 1)

            def y_hi(t, s):
                act.wait_ge(s_yz, t + 1)
                act.wait_ge(s_xo, t + 1)
                nc.scalar.activation(y16[:, 0:H, ds(t, 1), 0, :].rearrange("p h a f -> p h (a f)"),
                                     ps[:, 2 + s, :].rearrange("p (h f) -> p h f", h=H), ACT.Copy,
                                     scale=YS).then_inc(s_yhi, 1)

            def c_waits(t):
                if isinstance(t, int) and t < 2:
                    return []
                return [(s_xT, LN_A + t - 1)]

            def stage_c2(t, s, first, last):
                copy_hT(t, s, LN_A)
                if not last:
                    std_relu(t + 1, 1 - s, LN_A, x1, c_waits(t + 1))
                if not first:
                    y_hi(t - 1, 1 - s)

            act.wait_ge(s_wt, 2 * KT)
            std_relu(0, 0, LN_A, x1, [])
            in_pairs(act, stage_c2)
            y_hi(NT - 1, 1)

            act.wait_ge(s_yz, NT)
            def to16(t, s, first, last):
                if not (isinstance(t, int) and t < 2):
                    act.wait_ge(s_nb, t - 1)
                nc.scalar.activation(keep16[:, s, :, :], adjT[:, :, ds(t * P, P)], ACT.Copy).then_inc(s_k16, 1)
            in_pairs(act, to16)

        @block.vector
        def _(dve):
            def coefs(t, s, base, src, wait_src):
                wait_src(t, s)
                nc.vector.bn_stats(stats[:, s, :], src[:, s, :]).then_inc(s_bn, 1)
                dve.wait_ge(s_bn, base + t + 1)
                if not (isinstance(t, int) and t < 2 and base == 0):
                    dve.wait_ge(s_hn, base + t - 1)
                nc.vector.tensor_tensor(both[:, s, :], stats[:, s, 1:3], stats[:, s, 4:6], ALU.add)
                nc.vector.tensor_tensor(gap[:, s, 0:1], stats[:, s, 1:2], stats[:, s, 4:5], ALU.subtract) \
                  .then_inc(s_gap, 1)
                dve.wait_ge(s_gap, base + t + 1)
                nc.vector.scalar_tensor_tensor(out=gap[:, s, 1:2], in0=gap[:, s, 0:1], scalar=C / 4,
                                               in1=gap[:, s, 0:1], op0=ALU.mult, op1=ALU.mult).then_inc(s_gap2, 1)
                dve.wait_ge(s_gap2, base + t + 1)
                nc.vector.tensor_tensor(cvar[:, s:s + 1], both[:, s, 1:2], gap[:, s, 1:2], ALU.add).then_inc(s_mv, 1)
                dve.wait_ge(s_std, base + t + 1)
                nc.vector.reciprocal(rstd[:, s:s + 1], std[:, s:s + 1]).then_inc(s_rstd, 1)
                dve.wait_ge(s_rstd, base + t + 1)
                nc.vector.scalar_tensor_tensor(out=nbias[:, s:s + 1], in0=both[:, s, 0:1], scalar=-0.5,
                                               in1=rstd[:, s:s + 1], op0=ALU.mult, op1=ALU.mult).then_inc(s_coef, 1)

            def x_here(t, s):
                if not isinstance(t, int):
                    dve.wait_ge(s_x[s], (t - s) * (HALVES // 2) + HALVES)
                elif t == NT - 1:
                    dve.wait_ge(s_x[s], X_A[1])
                else:
                    dve.wait_ge(s_x[s], HALVES * (t // 2 + 1))

            def group(t, s, g, of, to):
                dve.wait_ge(of, NG * t + g + 1)
                nc.vector.tensor_copy(adjT[:, GO[g]:GO[g] + G[g], ds(t * P, P)],
                                      psb[:, 6 + g % 2, 0:G[g] * P].rearrange("p (j i) -> p j i", i=P)) \
                  .then_inc(to, 1)

            def stage_a(t, s, first, last):
                if not last:
                    coefs(t + 1, 1 - s, 0, xb, x_here)
                for g in range(NG):
                    group(t, s, g, s_g, s_gev)

            coefs(0, 0, 0, xb, x_here)
            dve.wait_ge(s_w0, HALVES)
            dve.wait_ge(s_av, 2 * HALVES)
            n = 0
            for a in range(2):
                for k in range(KT):
                    if n:
                        dve.wait_ge(s_wa, n)
                    nc.vector.tensor_tensor(hmean[:, :], W0[:, k, :], a_bc[:, a, :], ALU.mult).then_inc(s_wap, 1)
                    n += 1
                    dve.wait_ge(s_wap, n)
                    nc.vector.tensor_reduce(wa[:, k, a * H:(a + 1) * H], hmean[:, :].rearrange("p (h f) -> p h f", h=H),
                                            AX_X, ALU.add).then_inc(s_wa, 1)
            in_pairs(dve, stage_a)

            dve.wait_ge(s_hev, NT)
            dve.wait_ge(s_cast, NT)
            nc.vector.tensor_reduce(top[:, 0:H], sn[:, H:2 * H, :], AX_X, ALU.max).then_inc(s_top, 1)
            nc.vector.tensor_reduce(top[:, H:H + 1], cnt[:, :], AX_X, ALU.max).then_inc(s_top, 1)
            dve.wait_ge(s_topa, 1)
            tops = topa[:, 0:H].unsqueeze(2).to_broadcast([P, H, NT])
            nc.vector.tensor_tensor(r_i[:, :, :], sn[:, 0:H, :], tops, ALU.add).then_inc(s_nd1, 1)
            dve.wait_ge(s_nd1, 1)
            nc.vector.tensor_scalar(r_i[:, :, :], r_i[:, :, :], U_TOP, None, ALU.min).then_inc(s_nd, 1)
            nc.vector.tensor_tensor(Fj[:, :, :], sn[:, H:2 * H, :], tops, ALU.subtract).then_inc(s_nd, 1)
            nc.vector.tensor_scalar(flag[:, :], topa[:, H:H + 1], float(NEIGH), None, ALU.is_gt).then_inc(s_flag, 1)
            nc.vector.tensor_scalar(empty[:, :], cnt[:, :], 0.0, None, ALU.is_equal).then_inc(s_cn0, 1)
            nc.vector.tensor_scalar(some[:, :], cnt[:, :], 0.0, None, ALU.is_gt).then_inc(s_cn0, 1)
            nc.vector.tensor_scalar(rcnt[:, :], cnt[:, :], 1.0, float(NEIGH), ALU.max, ALU.min).then_inc(s_cn0, 1)
            dve.wait_ge(s_cn0, 3)
            nc.vector.reciprocal(rcnt[:, :], rcnt[:, :]).then_inc(s_cn0, 1)
            dve.wait_ge(s_exp, 2)
            nc.vector.tensor_scalar(nKj[:, :, :], Kj[:, :, :], -1.0, None, ALU.mult).then_inc(s_nk, 1)
            dve.wait_ge(s_cn0, 4)
            nc.vector.tensor_scalar(rcnt[:, :], rcnt[:, :], 1.0 / YS, None, ALU.mult).then_inc(s_cn0, 1)

            def p_step(h, c, j, s, first=False):
                step = (h * CHUNKS + c) * NT + j
                dve.wait_ge(s_q, step + 1)
                if not first:
                    dve.wait_ge(s_pe, step - 1)
                nc.vector.scalar_tensor_tensor(out=Pt[:, s, :], in0=q[:, s, :],
                                               scalar=Kj[:, ds(h, 1), ds(j, 1)].rearrange("p a b -> p (a b)"),
                                               in1=adjT[:, ds(j, 1), c * CW:(c + 1) * CW].rearrange("p a n -> p (a n)"),
                                               op0=ALU.add, op1=ALU.mult).then_inc(s_p, 1)

            def normalise(h, c):
                rnd = h * CHUNKS + c
                dve.wait_ge(s_pe, (rnd + 1) * NT)
                FULL = CT // TPB * TPB
                dens = ps[:, 0:CT // TPB, 0:TPB * FA].rearrange("p b (m f) -> p b m f", f=FA)[:, :, :, FH:FA]
                nc.vector.tensor_tensor(den[:, 0:FULL].rearrange("p (b m a) -> p b m a", m=TPB, a=1), dens,
                                        empty[:, c * CT:c * CT + FULL].rearrange("p (b m a) -> p b m a", m=TPB, a=1),
                                        ALU.add).then_inc(s_den, 1)
                for m in range(FULL, CT):
                    nc.vector.tensor_tensor(den[:, m:m + 1], acc(m)[:, FH:FA], empty[:, c * CT + m:c * CT + m + 1],
                                            ALU.add).then_inc(s_den, 1)
                dve.wait_ge(s_den, (rnd + 1) * (1 + CT - FULL))
                nc.vector.reciprocal(den[:, 0:CT], den[:, 0:CT]).then_inc(s_rden, 1)
                dve.wait_ge(s_rden, rnd + 1)
                for b in range(NB):
                    for m in range(b * TPB, min(b * TPB + TPB, CT)):
                        ins = nc.vector.tensor_scalar(
                            slots[:, ds(h, 1), c * CT + m, 0:FH].rearrange("p a f -> p (a f)"),
                            acc(m)[:, 0:FH], den[:, m:m + 1], None, ALU.mult)
                    ins.then_inc(s_ev, 1)

            def rounds(h, final):
                for c in range(CHUNKS):
                    p_step(h, c, 1, 1, first=isinstance(h, int) and h == 0 and c == 0)
                    with dve.Fori(1, NT // 2) as i:
                        for s in range(2):
                            p_step(h, c, i * 2 + s, s)
                    if c + 1 < CHUNKS:
                        p_step(h, c + 1, 0, 0)
                    elif not final:
                        p_step(h + 1, 0, 0, 0)
                    normalise(h, c)

            dve.wait_ge(s_g, GROUPS)
            dve.wait_ge(s_gev, GROUPS)
            dve.wait_ge(s_rtc, 1)
            p_step(0, 0, 0, 0, first=True)
            rounds(0, False)
            with dve.Fori(1, H - 1) as h:
                rounds(h, False)
            rounds(H - 1, True)

            many = dve.value_load(flag[0:1, 0:1], min_val=0, max_val=1)
            with dve.If(many > 0):
                def c1(t, s, first, last):
                    if isinstance(t, int):
                        dve.wait_ge(c_adj[s], X_A[1] if last else HALVES * (t // 2 + 1))
                    else:
                        dve.wait_ge(c_adj[s], (t - s) * (HALVES // 2) + HALVES)
                    if not first:
                        dve.wait_ge(c_dif, t)
                    nc.vector.tensor_tensor_scan(count[:, 1:N + 1], adj_i[:, s, 0:N], cap[:, 0:1].to_broadcast([P, N]),
                                                 0.0, ALU.add, ALU.min).then_inc(c_scan, 1)
                    dve.wait_ge(c_scan, t + 1)
                    if not (isinstance(t, int) and t < 2):
                        dve.wait_ge(c_g, NG * (t - 1))
                    nc.vector.tensor_tensor(adj_b[:, s, 0:N], count[:, 1:N + 1], count[:, 0:N],
                                            ALU.subtract).then_inc(c_dif, 1)
                    if not first:
                        for g in range(NG):
                            group(t - 1, 1 - s, g, c_g, c_gev)
                nc.vector.memset(adj_b[:, :, N:NP], 0.0).then_inc(c_zero, 1)
                nc.vector.memset(count[:, 0:1], 0.0).then_inc(c_zero, 1)
                dve.wait_ge(c_zero, 2)
                in_pairs(dve, c1)
                for g in range(NG):
                    group(NT - 1, 1, g, c_g, c_gev)
                dve.wait_ge(c_gev, GROUPS)

            for k in range(KT):
                dve.wait_ge(s_wt, 2 * k + 2)
                nc.vector.tensor_copy(wT[:, 1, k, :], ps[:, 2 * (k % 2) + 1, :]).then_inc(s_wtc[1], 1)

            def x1_here(t, s):
                dve.wait_ge(s_xo, t + 1)
                if not (isinstance(t, int) and t < 2):
                    dve.wait_ge(s_zo, t - 1)
                nc.vector.scalar_tensor_tensor(out=x1[:, s, :], in0=hmean[:, :],
                                               scalar=empty[:, ds(t, 1)], in1=xo[:, s, :], op0=ALU.mult,
                                               op1=ALU.add).then_inc(s_x1, 1)
                dve.wait_ge(s_x1, t + 1)

            def y_lo(t, s):
                dve.wait_ge(s_yhi, t + 1)
                nc.vector.scalar_tensor_tensor(
                    out=y16[:, 0:H, ds(t, 1), 1, :].rearrange("p h a f -> p h (a f)"),
                    in0=ps[:, 2 + s, :].rearrange("p (h f) -> p h f", h=H), scalar=YS,
                    in1=y16[:, 0:H, ds(t, 1), 0, :].rearrange("p h a f -> p h (a f)"),
                    op0=ALU.mult, op1=ALU.subtract).then_inc(s_ylo, 1)

            def leaky_z(t, s):
                dve.wait_ge(s_z, t + 1)
                nc.vector.tensor_tensor(zt[:, s, :], ps[:, 4 + s, :], bline, ALU.add).then_inc(s_zt, 1)
                dve.wait_ge(s_zt, t + 1)
                if not (isinstance(t, int) and t < 2):
                    dve.wait_ge(s_zo, t - 1)
                nc.vector.scalar_tensor_tensor(out=zl[:, s, :], in0=zt[:, s, :], scalar=SLOPE, in1=zt[:, s, :],
                                               op0=ALU.mult, op1=ALU.max).then_inc(s_zl, 1)

            def stage_c2(t, s, first, last):
                if not first:
                    leaky_z(t - 1, 1 - s)
                if not last:
                    coefs(t + 1, 1 - s, LN_A, x1, x1_here)
                if not first:
                    y_lo(t - 1, 1 - s)

            dve.wait_ge(s_bl, HALVES)
            dve.wait_ge(s_hmc, 1)
            coefs(0, 0, LN_A, x1, x1_here)
            in_pairs(dve, stage_c2)
            leaky_z(NT - 1, 1)
            y_lo(NT - 1, 1)

            dve.wait_ge(s_bnb, HALVES)
            dve.wait_ge(s_cn0, 5)

            def stage_d(t, s, first, last):
                dve.wait_ge(s_nb, t + 1)
                nc.vector.scalar_tensor_tensor(out=dt_[:, s, :], in0=ps[:, s, :], scalar=rcnt[:, ds(t, 1)], in1=bnb,
                                               op0=ALU.mult, op1=ALU.add).then_inc(s_dt, 1)
                dve.wait_ge(s_dt, t + 1)
                nc.vector.scalar_tensor_tensor(out=dl[:, s, :], in0=dt_[:, s, :], scalar=SLOPE, in1=dt_[:, s, :],
                                               op0=ALU.mult, op1=ALU.max).then_inc(s_dl, 1)
                dve.wait_ge(s_dl, t + 1)
                if isinstance(t, int):
                    dve.wait_ge(s_zin[s], HALVES * (t // 2 + 1))
                    if t >= 2:
                        dve.wait_ge(s_out[s], HALVES * (t // 2))
                else:
                    dve.wait_ge(s_zin[s], (t - s) * (HALVES // 2) + HALVES)
                    dve.wait_ge(s_out[s], (t - s) * (HALVES // 2))
                nc.vector.scalar_tensor_tensor(out=do[:, s, :], in0=dl[:, s, :], scalar=some[:, ds(t, 1)],
                                               in1=zin[:, s, :], op0=ALU.mult, op1=ALU.add).then_inc(s_do, 1)
            in_pairs(dve, stage_d)

        @block.tensor
        def _(pe):
            def transposes(t, s, base):
                pe.wait_ge(s_hn, base + t + 1)
                if not (isinstance(t, int) and t < 2):
                    pe.wait_ge(s_hT, base + t - 1)
                for k in range(KT):
                    ins = nc.tensor.transpose(ps[:, s, k * P:(k + 1) * P], hn[:, s, k * P:(k + 1) * P], ident[:, :])
                ins.then_inc(s_xT, 1)

            def group(t, s, g, ready, done, used):
                if g == 0:
                    pe.wait_ge(ready, t + 1)
                if not (isinstance(t, int) and t == 0 and g < 2):
                    pe.wait_ge(used, NG * t + g - 1)
                for b in range(G[g]):
                    j = GO[g] + b
                    ins = nc.tensor.transpose(psb[:, 6 + g % 2, b * P:(b + 1) * P], adj_b[:, s, j * P:(j + 1) * P],
                                              ident_b[:, :])
                ins.then_inc(done, 1)

            def product(t, s, k):
                if k == 0:
                    pe.wait_ge(s_hT, t + 1)
                    if not (isinstance(t, int) and t < 2):
                        pe.wait_ge(s_hev, t - 1)
                w = hT[:, s, k * P:(k + 1) * P]
                nc.tensor.matmul(ps[:, 2 + s, :], w, W0[:, k, :], start=(k == 0), stop=(k == KT - 1))
                ins = nc.tensor.matmul(ps[:, 4 + s, 0:2 * H], w, wa[:, k, :], start=(k == 0), stop=(k == KT - 1))
                if k == KT - 1:
                    ins.then_inc(s_mm, 1)

            def stage_a(t, s, first, last):
                transposes(t, s, 0)
                for g in range(NG):
                    group(t, s, g, s_cast, s_g, s_gev)
                    if not first:
                        product(t - 1, 1 - s, g)

            pe.wait_ge(s_const, 8)
            pe.wait_ge(s_w0, HALVES)
            pe.wait_ge(s_wa, 2 * KT)
            in_pairs(pe, stage_a)
            for k in range(KT):
                product(NT - 1, 1, k)

            pe.wait_ge(s_hsum, NT)
            pe.wait_ge(s_hT, NT)
            for k in range(KT):
                ins = nc.tensor.matmul(ps[:, 1, k * P:(k + 1) * P], hsum[:, k * P:(k + 1) * P], ones[:, :],
                                       start=True, stop=True)
            ins.then_inc(s_hst, 1)
            pe.wait_ge(s_exp, 1)
            nc.tensor.transpose(ps[0:H * NT, 0, 0:P], r_i[:, :, :].rearrange("p h t -> p (h t)"), ident[:, :]) \
              .then_inc(s_rt, 1)
            pe.wait_ge(s_hstc, 1)
            pe.wait_ge(s_hev, NT)
            for k in range(KT):
                ins = nc.tensor.matmul(ps[:, 2, :], hsumT[:, k, :], W0[:, k, :], start=(k == 0), stop=(k == KT - 1))
            ins.then_inc(s_hm, 1)
            pe.wait_ge(s_hmc, 1)

            def step(h, c, j, s):
                fst, lst = isinstance(j, int) and j == 0, isinstance(j, int) and j == NT - 1
                pe.wait_ge(s_p, (h * CHUNKS + c) * NT + j + 1)
                for m in range(CT):
                    if fst and m % TPB == 0 and not (isinstance(h, int) and h == 0 and c == 0):
                        pe.wait_ge(s_ev, (h * CHUNKS + (c - 1)) * NB + m // TPB + 1)
                    ins = nc.tensor.matmul(acc(m), Pt[:, s, m * P:(m + 1) * P],
                                           slots[:, ds(h + 1, 1), ds(j, 1), :].rearrange("p a b f -> p (a b f)"),
                                           start=(fst and m % TPB == 0), stop=lst, skip_group_check=True)
                ins.then_inc(s_pe, 1)

            def rounds(h):
                for c in range(CHUNKS):
                    for s in range(2):
                        step(h, c, s, s)
                    with pe.Fori(1, NT // 2 - 1) as i:
                        for s in range(2):
                            step(h, c, i * 2 + s, s)
                    for s in range(2):
                        step(h, c, NT - 2 + s, s)

            rounds(0)
            with pe.Fori(1, H) as h:
                rounds(h)
            pe.wait_ge(s_ev, H * CHUNKS * NB)

            many = pe.value_load(flag[0:1, 0:1], min_val=0, max_val=1)
            with pe.If(many > 0):
                def c1(t, s, first, last):
                    for g in range(NG):
                        group(t, s, g, c_dif, c_g, c_gev)
                in_pairs(pe, c1)

            pe.wait_ge(s_wnb, HALVES)
            pe.wait_ge(s_wl, HALVES)
            for k in range(KT):
                for w, raw in enumerate((w_nb_raw, w_line_raw)):
                    if k >= 2:
                        pe.wait_ge(s_wtc[w], k - 1)
                    for o in range(KT):
                        ins = nc.tensor.transpose(ps[:, 2 * (k % 2) + w, o * P:(o + 1) * P],
                                                  raw[:, o, k * P:(k + 1) * P], ident[:, :])
                    ins.then_inc(s_wt, 1)

            def products(t, s):
                pe.wait_ge(s_hT, LN_A + t + 1)
                if not (isinstance(t, int) and t < 2):
                    pe.wait_ge(s_ylo, t - 1)
                    pe.wait_ge(s_zt, t - 1)
                for w in (1, 0):
                    for k in range(KT):
                        ins = nc.tensor.matmul(ps[:, 2 + 2 * w + s, :], hT[:, s, k * P:(k + 1) * P], wT[:, w, k, :],
                                               start=(k == 0), stop=(k == KT - 1))
                    ins.then_inc(s_z if w else s_yz, 1)

            def stage_c2(t, s, first, last):
                transposes(t, s, LN_A)
                if not first:
                    products(t - 1, 1 - s)

            for w in range(2):
                pe.wait_ge(s_wtc[w], KT)
            in_pairs(pe, stage_c2)
            products(NT - 1, 1)

            pe.wait_ge(s_ylo, NT)
            def stage_d(t, s, first, last):
                pe.wait_ge(s_k16, t + 1)
                if not (isinstance(t, int) and t < 2):
                    pe.wait_ge(s_dt, t - 1)
                for j in range(NT):
                    for part in range(2):
                        ins = nc.tensor.matmul(ps[:, s, :], keep16[:, s, j, :], y16[:, 0:H, j, part, :],
                                               start=(j == 0 and part == 0), stop=(j == NT - 1 and part == 1))
                ins.then_inc(s_nb, 1)
            in_pairs(pe, stage_d)


_INS = ['x', 'adj', 'L0_gnn_W', 'L0_gnn_a_self', 'L0_gnn_a_neighs', 'L1_gnn_W_nb', 'L1_gnn_b_nb', 'L1_gnn_W_line',
        'L1_gnn_b_line']


def kernel(**inputs):
    import numpy as _np
    import concourse.bacc as _bacc
    from concourse import mybir as _mybir
    from concourse.bass_utils import run_bass_kernel_spmd as _run

    nc = _bacc.Bacc("TRN2", target_bir_lowering=False, num_devices=1)
    arrays, args = {}, []
    for name in _INS:
        a = _np.ascontiguousarray(inputs[name])
        arrays[f"in_{name}_dram"] = a
        args.append(nc.dram_tensor(f"in_{name}_dram", a.shape, _mybir.dt.from_np(a.dtype), kind="ExternalInput").ap())
    args.append(nc.dram_tensor("out_0_dram", inputs['x'].shape, _mybir.dt.float32, kind="ExternalOutput").ap())
    gnn_two_layers(nc, *args)
    r = _run(nc, [arrays], core_ids=[0])
    return r.results[0]["out_0_dram"]
```

```python
from contextlib import ExitStack

import concourse.bass as bass
from concourse import mybir

F32 = mybir.dt.float32
F16 = mybir.dt.float16
BF16 = mybir.dt.bfloat16
I32 = mybir.dt.int32
U16 = mybir.dt.uint16
U8 = mybir.dt.uint8
ALU = mybir.AluOpType
ACT = mybir.ActivationFunctionType
AX_X = mybir.AxisListType.X
ds = bass.ds


def gnn_two_layers(nc, x, adj, W, a_self, a_neighs, W_nb, b_nb, W_line, b_line, out):
    N, C = x.shape
    P = 128
    Q = -(-N // (2 * P))
    NT = 2 * Q
    NP = NT * P
    LAST = N // 2 - (Q - 1) * P
    KT = C // P
    H, FH = a_self.shape[1], a_self.shape[2]
    FA = FH + 1
    CW = Q * P
    NEIGH = 64
    ALPHA = 0.2
    SLOPE = 0.01
    EPS = 1e-5
    EDGE = 192
    KEEP = 64.0
    XS = 2048.0
    WS = 256.0
    YS = 128.0
    U_TOP = 100.0
    HALVES = 16
    HB = [7, 6]
    HS = [0, HB[0]]
    HC = [(0, HB[0] * 2 * P), (HB[0] * 2 * P, N)]
    UNITS_A = NT
    UNITS = 2 * NT
    assert sum(HB) == Q and H * FH == C == 512 and N % 2 == 1
    ROWS = [(0, LAST // 16 * 16), (LAST // 16 * 16, LAST)]
    NR = len(ROWS)

    r_dram = nc.dram_tensor("r_rows", [H * NT, P], F32, kind="Internal").ap()
    r_flat = r_dram.rearrange("(a t) p -> a (t p)", a=1)
    z_dram = nc.dram_tensor("z_rows", [NP, C], F32, kind="Internal").ap()

    def node_rows(m, i, s, c0, c1, a=0, b=P):
        if isinstance(i, int):
            first = 2 * P * i + s + 2 * a
            return m[first:first + 2 * (b - a) - 1:2, c0:c1]
        rows = m[s:s + 2 * P * (Q - s) - 1:2, c0:c1].rearrange("(q m) c -> q m c", m=P)
        return rows[ds(i, 1)].rearrange("q m c -> (q m) c")

    def nxt(i, s):
        return (i, 1) if s == 0 else (i + 1, 0)

    def prv(i, s):
        return (i, 0) if s == 1 else (i - 1, 1)

    def has_nxt2(i):
        return not (isinstance(i, int) and i == Q - 1)

    with ExitStack() as ctx:
        def sb(name, shape, dt):
            return ctx.enter_context(nc.sbuf_tensor(name, shape, dt))

        def sem(name):
            return ctx.enter_context(nc.semaphore(name))

        adjT = sb("adjT", [P, Q, NP, 2], U8)
        adjT16 = adjT[:, :, :, :].rearrange("p q n b -> p q (n b)").bitcast(U16)
        slots = sb("slots", [P, H + 1, NT, FA], F32)
        flat_slots = slots[:, :, :, :].rearrange("p s t f -> p s (t f)")
        work = sb("work", [P, 6 * CW], F32)
        aux = sb("aux", [P, 6 * C], F32)

        def view(region, at, *shape, dt=F32):
            per = {F32: 1, I32: 1, F16: 2, U8: 4, BF16: 2}[dt]
            n = 1
            for k in shape:
                n *= k
            v = region[:, at:at + -(-n // per)].bitcast(dt)[:, 0:n]
            names = "abcd"[:len(shape)]
            return v.rearrange(f"p ({' '.join(names)}) -> p {' '.join(names)}", **dict(zip(names, shape)))

        adj_i = view(flat_slots[:, 0, :], 0, NP, dt=I32)
        W_raw = view(work, 0, KT, C)
        a_bc = view(work, KT * C, 2, C)
        r_T = work[0:H * NT, 2 * CW:2 * CW + P]
        hsum16 = view(work, 3 * CW, 2, KT, P, dt=F16)
        adj8_a = view(work, 4 * CW - NP // 4, NP, dt=U8)
        W16 = view(work, 4 * CW, 2, KT, C, dt=F16)
        hsum = view(work, 4 * CW + KT * C, C)
        R = view(work, 0, 2, CW)
        q = view(work, 2 * CW, 2, CW)
        Pt = view(work, 4 * CW, 2, CW)
        adj8_b = view(aux, 0, NP, dt=U8)
        w_nb_raw = view(aux, 2 * C, KT, C)
        c_adj = view(work, 0, NP, dt=I32)
        c_keep8 = view(work, NP, NP, dt=U8)
        count = view(flat_slots[:, H, :], KT * C, NP + 4, dt=U8)
        w_line_raw = view(flat_slots[:, H, :], 0, KT, C)
        wT16 = view(work, 0, 2, 2, KT, C, dt=F16)
        at = 2 * KT * C
        zt, zl, zo = (view(work, at + 2 * C * k, 2, C) for k in range(3))
        bline = view(work, at + 6 * C, C)
        xb = view(aux, 0, 2, C)
        hn = view(aux, 2 * C, 2, C)
        hT16 = view(aux, 4 * C, 2, 2, C, dt=F16)
        keep16 = view(work, 0, 2, NT, P, dt=F16)
        zin, dt_, dl, do = (view(work, NP + 2 * C * k, 2, C) for k in range(4))
        bnb = view(work, NP + 8 * C, C)
        y16 = slots[:, :, :, 0:FH].bitcast(F16).rearrange("p s t (a f) -> p s t a f", a=2)

        hmean = sb("hmean", [P, C], F32)
        wa = sb("wa", [P, KT, 2 * H], F32)
        wa16 = sb("wa16", [P, 2, KT, 2 * H], F16)
        ident = sb("ident", [P, P], F32)
        ident_b = sb("ident_b", [P, P], BF16)
        ones = sb("ones", [P, P], F32)
        eps = sb("eps", [P, 1], F32)
        cap = sb("cap", [P, 1], F32)
        stats = sb("stats", [P, 2, 6], F32)
        both = sb("both", [P, 2, 2], F32)
        gap = sb("gap", [P, 2, 2], F32)
        cvar = sb("cvar", [P, 2], F32)
        std = sb("std", [P, 2], F32)
        rstd = sb("rstd", [P, 2], F32)
        nbias = sb("nbias", [P, 2], F32)
        sn = sb("sn", [P, 2 * H, NT], F32)
        cnt2 = sb("cnt2", [P, NT, 2], F32)
        rcnt = sb("rcnt", [P, NT], F32)
        top = sb("top", [P, H + 1], F32)
        topa = sb("topa", [P, H + 1], F32)
        Fj = sb("Fj", [P, H, NT], F32)
        r_i = sb("r_i", [P, H, NT], F32)
        Kj = sb("Kj", [P, H, NT], F32)
        nKj = r_i
        flag = sb("flag", [P, 1], I32)
        empty = sb("empty", [P, NT], F32)
        some = sb("some", [P, NT], F32)
        den = sb("den", [P, Q], F32)
        ps = ctx.enter_context(nc.psum_tensor("ps", [P, 8, C], F32))
        psb = ps[:, :, :].bitcast(BF16)
        psw = ps[:, :, :].bitcast(U16)
        TPB = 3
        NB = -(-Q // TPB)

        BANKS = [[2, 3, 4, 0, 1], [5, 6, 7, 0, 1]]
        OWN = 3

        def acc(c, m):
            return ps[:, BANKS[c][m // TPB], (m % TPB) * FA:(m % TPB + 1) * FA]

        def tile_of(a, L):
            return a[:, 0:H, ds(L, 1), 0:FH].rearrange("p h a f -> p h (a f)")

        def by_head(v):
            return v.rearrange("p (h f) -> p h f", h=H)

        s_x = [sem(f"x_loaded{s}") for s in range(2)]
        s_adj = [sem(f"adj_half{s}_loaded") for s in range(2)]
        s_w0 = sem("w0_loaded")
        s_av = sem("a_loaded")
        s_const = sem("consts_set")
        s_xpad = sem("x_pad_row_zeroed")
        s_apad = sem("adj_pad_rows_zeroed")
        s_cpad = sem("adj8_b_pad_column_zeroed")
        s_bn = sem("bn_stats_done")
        s_gap = sem("mean_gap_done")
        s_gap2 = sem("mean_gap_squared")
        s_mv = sem("variance_done")
        s_std = sem("std_done")
        s_rstd = sem("rstd_done")
        s_coef = sem("ln_coefs_done")
        s_hn = sem("hn_done")
        s_hs0 = sem("hsum_zeroed")
        s_hsum = sem("hsum_added")
        s_wap = sem("wa_product_done")
        s_wa = sem("wa_done")
        s_wh = sem("w_high_done")
        s_wl16 = sem("w_and_wa_parts_done")
        s_cast = sem("adj_half_cast")
        s_xT = sem("x_transposed")
        s_hi = sem("hT_high_done")
        s_lo = sem("hT_low_done")
        s_mm = sem("h_product_done")
        s_hev = sem("h_copied")
        s_g = sem("adj_half_transposed")
        s_gev = sem("adj_half_copied")
        s_top = sem("tops_done")
        s_topa = sem("tops_all_done")
        s_nd1 = sem("u_added")
        s_nd = sem("shifted_scores_done")
        s_exp = sem("exps_done")
        s_nk = sem("minus_k_done")
        s_rt = sem("r_transposed")
        s_rtc = sem("rT_copied")
        s_rout = sem("r_stored")
        s_R = [sem(f"R_loaded{c}") for c in range(2)]
        s_cn = sem("count_steps_done")
        s_ctop = sem("count_top_done")
        s_ctopa = sem("count_top_all_done")
        s_flag = sem("flag_done")
        s_hst = sem("hsum_transposed")
        s_hsh = sem("hsum_high_done")
        s_hsl = sem("hsum_low_done")
        s_hm = sem("hmean_product_done")
        s_hmc = sem("hmean_done")
        s_q = sem("q_ready")
        s_p = sem("p_ready")
        s_pe = sem("p_consumed")
        s_den = sem("den_done")
        s_rden = sem("rden_done")
        s_ev = sem("bank_copied")
        c_adjs = sem("c1_adj_loaded")
        c_pad = sem("c1_pad_zeroed")
        c_zero = sem("c1_zeros_set")
        c_scan = sem("c1_scan_done")
        c_dif = sem("c1_difference_done")
        c_keep = sem("c1_keep_done")
        c_g = sem("c1_half_transposed")
        c_gev = sem("c1_half_copied")
        s_wnb = sem("w_nb_loaded")
        s_wl = sem("w_line_loaded")
        s_bl = sem("b_line_loaded")
        s_bnb = sem("b_nb_loaded")
        s_wt = sem("w_transposed")
        s_wtc = [sem("wT_high_done"), sem("wT_low_done")]
        s_x2 = [sem(f"x_again_loaded{s}") for s in range(2)]
        s_xo = sem("x_added")
        s_x1 = sem("x1_done")
        s_z = sem("z_product_done")
        s_yz = sem("y_product_done")
        s_yhi = sem("y_high_done")
        s_ylo = sem("y_low_done")
        s_zt = sem("z_biased")
        s_zl = sem("z_leaky")
        s_zo = sem("z_done")
        s_zs = [sem(f"z_stored{s}") for s in range(2)]
        s_k16 = sem("keep16_done")
        s_nb = sem("neighbour_sums_done")
        s_dt = sem("mean_biased")
        s_dl = sem("mean_leaky")
        s_do = sem("out_tile_done")
        s_zin = [sem(f"z_loaded{s}") for s in range(2)]
        s_out = [sem(f"out_stored{s}") for s in range(2)]

        LN_A = NT
        STEPS = H * 2 * NT

        def in_pairs(eng, body, stop=Q, peel=1):
            end = stop - peel if stop == Q else stop
            for i in range(peel):
                for s in range(2):
                    body(i, s, i == 0 and s == 0, False)
            with eng.Fori(peel, end) as i:
                for s in range(2):
                    body(i, s, False, False)
            for i in range(end, stop):
                for s in range(2):
                    body(i, s, False, i == Q - 1 and s == 1)

        def early(i):
            return isinstance(i, int) and i == 0

        def is_last(i, s):
            return isinstance(i, int) and i == Q - 1 and s == 1

        def loaded(i, s):
            return HALVES * (Q - 1 + NR) if is_last(i, s) else i * HALVES + HALVES

        block = ctx.enter_context(nc.Block())

        @block.sync
        def _(sp):
            def load_x(i, s, semaphore):
                for a, b in ROWS if is_last(i, s) else [(0, P)]:
                    sp.dma_start(xb[a:b, s, :], node_rows(x, i, s, 0, C, a, b)).then_inc(semaphore[s], HALVES)

            def load_adj(i, b, g):
                c0, c1 = HC[g]
                for r0, r1 in ROWS if is_last(i, b) else [(0, P)]:
                    sp.dma_start(adj_i[r0:r1, c0:c1], node_rows(adj, i, b, c0, c1, r0, r1)) \
                      .then_inc(s_adj[g], HALVES)

            def stage_a(i, s, first, last):
                if not last:
                    ni, ns = nxt(i, s)
                    if not first:
                        sp.wait_ge(s_hn, i * 2 + s)
                    if is_last(ni, ns):
                        sp.wait_ge(s_xpad, 1)
                    load_x(ni, ns, s_x)
                if not early(i):
                    sp.wait_ge(s_cast, i * 2 + s - 1)
                load_adj(i, 0, s)

            load_x(0, 0, s_x)
            sp.dma_start(W_raw, W.rearrange("(k p) n -> p k n", p=P)).then_inc(s_w0, HALVES)
            for k, a in enumerate((a_self, a_neighs)):
                sp.dma_start(a_bc[:, k, :], a.rearrange("a h f -> a (h f)").to_broadcast([P, C])).then_inc(s_av, HALVES)
            in_pairs(sp, stage_a, peel=2)

            def load_r(h, c):
                sp.dma_start(R[:, c, :], r_flat[:, ds(h * NP + c * CW, CW)].to_broadcast([P, CW])) \
                  .then_inc(s_R[c], HALVES)

            def stage_b_adj(i, g):
                sp.wait_ge(s_cast, i * 2 + UNITS_A + g - 1)
                if is_last(i, 1):
                    sp.wait_ge(s_apad, g + 1)
                load_adj(i, 1, g)

            for g in range(2):
                stage_b_adj(0, g)
            sp.wait_ge(s_rtc, 1)
            sp.dma_start(r_dram, r_T).then_inc(s_rout, HALVES)
            sp.wait_ge(s_rout, HALVES)
            sp.wait_ge(s_wa, 2 * KT)
            sp.wait_ge(s_wl16, 4)
            for c in range(2):
                load_r(0, c)
            sp.wait_ge(s_mm, NT)
            sp.wait_ge(s_hsum, NT)
            sp.dma_start(w_nb_raw, W_nb.rearrange("(k p) n -> p k n", p=P)).then_inc(s_wnb, HALVES)
            with sp.Fori(1, Q - 1) as i:
                for g in range(2):
                    stage_b_adj(i, g)
            for g in range(2):
                stage_b_adj(Q - 1, g)
            with sp.Fori(1, H) as h:
                for c in range(2):
                    sp.wait_ge(s_q, (h * 2 + (c - 1)) * NT)
                    load_r(h, c)
            sp.wait_ge(s_g, UNITS)
            load_x(0, 0, s_x2)
            load_x(0, 1, s_x2)
            sp.wait_ge(s_pe, STEPS)
            sp.dma_start(w_line_raw, W_line.rearrange("(k p) n -> p k n", p=P)).then_inc(s_wl, HALVES)

            sp.wait_ge(s_flag, 1)
            many = sp.value_load(flag[0:1, 0:1], min_val=0, max_val=1)
            with sp.If(many > 0):
                def c1(i, b, first, last):
                    if not first:
                        sp.wait_ge(c_scan, i * 2 + b)
                    if last:
                        sp.wait_ge(c_pad, 1)
                    for r0, r1 in ROWS if last else [(0, P)]:
                        sp.dma_start(c_adj[r0:r1, 0:N], node_rows(adj, i, b, 0, N, r0, r1)).then_inc(c_adjs, HALVES)
                in_pairs(sp, c1)
                sp.wait_ge(c_gev, UNITS)

            sp.wait_ge(s_ev, H * 2 * NB)
            sp.dma_start(bline, b_line.rearrange("(a n) -> a n", a=1).to_broadcast([P, C])).then_inc(s_bl, HALVES)

            def reload(i, s, first, last):
                if not early(i):
                    sp.wait_ge(s_xo, i * 2 + s - 1)
                    load_x(i, s, s_x2)

            in_pairs(sp, reload)

            sp.wait_ge(s_zt, NT)
            sp.wait_ge(s_yz, NT)
            for s in range(2):
                sp.wait_ge(s_zs[s], HALVES * Q)
            sp.dma_start(bnb, b_nb.rearrange("(a n) -> a n", a=1).to_broadcast([P, C])).then_inc(s_bnb, HALVES)

            def store_out(i, s):
                sp.wait_ge(s_do, i * 2 + s + 1)
                for a, b in ROWS if is_last(i, s) else [(0, P)]:
                    sp.dma_start(node_rows(out, i, s, 0, C, a, b), do[a:b, s, :]).then_inc(s_out[s], HALVES)

            def stage_d(i, s, first, last):
                if not early(i):
                    sp.wait_ge(s_do, i * 2 + s - 1)
                sp.dma_start(zin[:, s, :], z_dram[ds((i + s * Q) * P, P), :]).then_inc(s_zin[s], HALVES)
                if not first:
                    store_out(*prv(i, s))

            in_pairs(sp, stage_d)
            store_out(Q - 1, 1)
            for s in range(2):
                sp.wait_ge(s_out[s], loaded(Q - 1, s))

        @block.gpsimd
        def _(pool):
            nc.gpsimd.memset(ident[:, :], 0.0).then_inc(s_const, 1)
            nc.gpsimd.memset(ones[:, :], 1.0).then_inc(s_const, 1)
            nc.gpsimd.memset(eps[:, :], EPS).then_inc(s_const, 1)
            nc.gpsimd.memset(cap[:, :], float(NEIGH)).then_inc(s_const, 1)
            nc.gpsimd.memset(adj8_a[:, N:NP], 0).then_inc(s_const, 1)
            pool.wait_ge(s_const, 5)
            nc.gpsimd.affine_select(out=ident[:, :], in_=ident[:, :], compare_op=ALU.not_equal, fill=1.0, base=0,
                                    pattern=[[-1, P]], channel_multiplier=1).then_inc(s_const, 1)
            pool.wait_ge(s_const, 6)
            nc.gpsimd.tensor_copy(ident_b[:, :], ident[:, :]).then_inc(s_const, 1)
            nc.gpsimd.memset(slots[:, 1:H + 1, :, FH:FA], 1.0).then_inc(s_const, 1)
            nc.gpsimd.memset(hsum, 0.0).then_inc(s_hs0, 1)
            pool.wait_ge(s_hs0, 1)

            def sum_h(i, s, first, last):
                pool.wait_ge(s_hn, i * 2 + s + 1)
                if not first:
                    pool.wait_ge(s_hsum, i * 2 + s)
                nc.gpsimd.tensor_tensor(hsum, hsum, hn[:, s, :], ALU.add).then_inc(s_hsum, 1)

            in_pairs(pool, sum_h, stop=Q - 1)
            pool.wait_ge(s_hsum, NT - 2)
            nc.gpsimd.memset(xb[P - 32:P, 1, :], 0.0).then_inc(s_xpad, 1)
            pool.wait_ge(s_xpad, 1)
            sum_h(Q - 1, 0, False, False)
            sum_h(Q - 1, 1, False, True)
            pool.wait_ge(s_hsum, NT)
            nc.gpsimd.memset(adj8_b[:, N:NP], 0).then_inc(s_cpad, 1)

            pool.wait_ge(s_top, 1)
            nc.gpsimd.partition_all_reduce(topa[:, 0:H], top[:, 0:H], P, bass.bass_isa.ReduceOp.max) \
              .then_inc(s_topa, 1)
            pool.wait_ge(s_topa, 1)
            for g, (c0, c1) in enumerate(HC):
                pool.wait_ge(s_cast, UNITS - 3 + g)
                nc.gpsimd.memset(adj_i[P - 32:P, c0:c1], 0).then_inc(s_apad, 1)
                pool.wait_ge(s_apad, g + 1)
            pool.wait_ge(s_ctop, 1)
            nc.gpsimd.partition_all_reduce(topa[:, H:H + 1], top[:, H:H + 1], P, bass.bass_isa.ReduceOp.max) \
              .then_inc(s_ctopa, 1)

            pool.wait_ge(s_pe, STEPS)
            pool.wait_ge(s_ev, H * 2 * NB)
            pool.wait_ge(s_flag, 1)
            many = pool.value_load(flag[0:1, 0:1], min_val=0, max_val=1)
            with pool.If(many > 0):
                pool.wait_ge(c_scan, NT - 1)
                nc.gpsimd.memset(c_adj[P - 32:P, :], 0).then_inc(c_pad, 1)
                pool.wait_ge(c_gev, UNITS)

            def add_x(i, s):
                pool.wait_ge(s_x2[s], loaded(i, s))
                o = tile_of(slots, i + s * Q)
                nc.gpsimd.tensor_tensor(o, by_head(xb[:, s, :]), o, ALU.add).then_inc(s_xo, 1)

            def add_z(i, s):
                pool.wait_ge(s_zl, i * 2 + s + 1)
                if not early(i):
                    pool.wait_ge(s_zs[s], i * HALVES)
                nc.gpsimd.tensor_tensor(by_head(zo[:, s, :]), by_head(zl[:, s, :]), tile_of(slots, i + s * Q),
                                        ALU.add).then_inc(s_zo, 1)

            def stage_c2(i, s, first, last):
                if has_nxt2(i) and not is_last(*nxt(i, s)) and not (isinstance(i, int) and i == Q - 2 and s == 1):
                    add_x(*nxt(i + 1, s))
                if not first:
                    add_z(*prv(i, s))

            for t in range(3):
                add_x(t // 2, t % 2)
            in_pairs(pool, stage_c2, peel=2)
            add_z(Q - 1, 1)

        @block.scalar
        def _(act):
            def std_(i, s, base):
                act.wait_ge(s_mv, i * 2 + s + (base + 1))
                nc.scalar.activation(std[:, s:s + 1], cvar[:, s:s + 1], ACT.Sqrt, bias=eps[:, 0:1],
                                     scale=1.0 / C).then_inc(s_std, 1)

            def relu(i, s, base, src, semaphores):
                t = i * 2 + s
                act.wait_ge(s_coef, t + (base + 1))
                if not early(i):
                    for sm, v in semaphores:
                        act.wait_ge(sm, t + (v - 1))
                nc.scalar.activation(by_head(hn[:, s, :]), src(i, s), ACT.Relu, bias=nbias[:, s:s + 1],
                                     scale=rstd[:, s:s + 1]).then_inc(s_hn, 1)

            def cast(i, g, b, dst):
                u = i * 2 + g + b * UNITS_A
                c0, c1 = HC[g]
                if is_last(i, b):
                    act.wait_ge(s_adj[g], HALVES * (2 * Q - 1 + NR))
                else:
                    act.wait_ge(s_adj[g], i * HALVES + (b * Q + 1) * HALVES)
                if b or not early(i):
                    act.wait_ge(s_g, u - 1)
                nc.scalar.activation(dst[:, c0:c1], adj_i[:, c0:c1], ACT.Copy, scale=float(EDGE),
                                     accum_out=cnt2[:, ds(i + b * Q, 1), g]).then_inc(s_cast, 1)

            def hT_high(i, s, base):
                t = i * 2 + s
                act.wait_ge(s_xT, t + (base + 1))
                if not early(i):
                    act.wait_ge(s_mm if base == 0 else s_yz, t - 1)
                nc.scalar.activation(hT16[:, s, 0, :], ps[:, s, :], ACT.Copy, scale=XS).then_inc(s_hi, 1)

            def x_src(i, s):
                return by_head(xb[:, s, :])

            a_used = [(s_xT, 0), (s_hsum, 0)]

            def stage_a(i, s, first, last):
                hT_high(i, s, 0)
                if not last:
                    relu(*nxt(i, s), 0, x_src, a_used)
                cast(i, s, 0, adj8_a)
                if has_nxt2(i):
                    std_(i + 1, s, 0)

            act.wait_ge(s_const, 8)
            std_(0, 0, 0)
            relu(0, 0, 0, x_src, a_used)
            std_(0, 1, 0)
            act.wait_ge(s_w0, HALVES)
            nc.scalar.activation(W16[:, 0, :, :], W_raw, ACT.Copy, scale=WS).then_inc(s_wh, 1)
            in_pairs(act, stage_a, peel=2)

            act.wait_ge(s_nd, 2)
            nc.scalar.activation(r_i[:, :, :], r_i[:, :, :], ACT.Exp, scale=1.0 - ALPHA).then_inc(s_exp, 1)
            nc.scalar.activation(Kj[:, :, :], Fj[:, :, :], ACT.Exp, scale=ALPHA).then_inc(s_exp, 1)
            act.wait_ge(s_exp, 2)
            nc.scalar.activation(Fj[:, :, :], Fj[:, :, :], ACT.Exp).then_inc(s_exp, 1)
            act.wait_ge(s_rt, 1)
            nc.scalar.activation(r_T, ps[0:H * NT, 0, 0:P], ACT.Copy).then_inc(s_rtc, 1)
            act.wait_ge(s_hst, 1)
            nc.scalar.activation(hsum16[:, 0, :, :], ps[:, 1, :].rearrange("p (k n) -> p k n", k=KT), ACT.Copy,
                                 scale=XS / N).then_inc(s_hsh, 1)
            act.wait_ge(s_hm, 1)
            nc.scalar.activation(hmean[:, :], ps[:, 2, :], ACT.Copy, scale=1.0 / (XS * WS)).then_inc(s_hmc, 1)

            act.wait_ge(s_nk, 1)
            act.wait_ge(s_exp, 3)
            act.wait_ge(s_rout, HALVES)
            act.wait_ge(s_g, UNITS_A)
            act.wait_ge(s_cpad, 1)

            def q_step(h, c, i, s, first=False):
                L = i + s * Q
                if not first:
                    act.wait_ge(s_p, h * (2 * NT) + i * 2 + (c * NT + s - 1))
                nc.scalar.activation(q[:, s, :], R[:, c, :], ACT.Relu,
                                     bias=nKj[:, ds(h, 1), ds(L, 1)].rearrange("p a b -> p (a b)"),
                                     scale=Fj[:, ds(h, 1), ds(L, 1)].rearrange("p a b -> p (a b)")).then_inc(s_q, 1)

            act.wait_ge(s_R[0], HALVES)
            for s in range(2):
                q_step(0, 0, 0, s, first=True)
                cast(0, s, 1, adj8_b)
            with act.Fori(1, Q - 1) as i:
                for s in range(2):
                    q_step(0, 0, i, s)
                    cast(i, s, 1, adj8_b)
            for s in range(2):
                q_step(0, 0, Q - 1, s)
                cast(Q - 1, s, 1, adj8_b)
            act.wait_ge(s_R[1], HALVES)
            with act.Fori(0, Q) as i:
                for s in range(2):
                    q_step(0, 1, i, s)
            with act.Fori(1, H) as h:
                for c in range(2):
                    act.wait_ge(s_R[c], h * HALVES + HALVES)
                    with act.Fori(0, Q) as i:
                        for s in range(2):
                            q_step(h, c, i, s)

            act.wait_ge(s_pe, STEPS)
            act.wait_ge(s_ev, H * 2 * NB)
            act.wait_ge(s_flag, 1)
            many = act.value_load(flag[0:1, 0:1], min_val=0, max_val=1)
            with act.If(many > 0):
                act.wait_ge(c_gev, UNITS)
            for k in range(KT):
                for w in range(2):
                    act.wait_ge(s_wt, 2 * k + w + 1)
                    nc.scalar.activation(wT16[:, w, 0, k, :], ps[:, 2 * (k % 2) + w, :], ACT.Copy, scale=WS) \
                      .then_inc(s_wtc[0], 1)

            def y_high(i, s):
                act.wait_ge(s_yz, i * 2 + s + 1)
                act.wait_ge(s_zo, i * 2 + s + 1)
                act.dma_start(z_dram[ds((i + s * Q) * P, P), :], zo[:, s, :]).then_inc(s_zs[s], HALVES)
                nc.scalar.activation(y16[:, 0:H, ds(i + s * Q, 1), 0, :].rearrange("p h a f -> p h (a f)"),
                                     by_head(ps[:, 2 + s, :]), ACT.Copy, scale=YS / (XS * WS)).then_inc(s_yhi, 1)

            def x1_src(i, s):
                return tile_of(slots, i + s * Q)

            def stage_c2(i, s, first, last):
                hT_high(i, s, LN_A)
                if not early(i):
                    y_high(i - 1, s)
                if has_nxt2(i):
                    std_(i + 1, s, LN_A)
                if not last:
                    relu(*nxt(i, s), LN_A, x1_src, [(s_xT, LN_A)])

            act.wait_ge(s_wt, 2 * KT)
            std_(0, 0, LN_A)
            relu(0, 0, LN_A, x1_src, [(s_xT, LN_A)])
            std_(0, 1, LN_A)
            in_pairs(act, stage_c2, peel=2)
            for s in range(2):
                y_high(Q - 1, s)

            act.wait_ge(s_yz, NT)

            def to16(i, s, first, last):
                if not early(i):
                    act.wait_ge(s_nb, i * 2 + s - 1)
                nc.scalar.activation(keep16[:, s, :, :].rearrange("p (q b) i -> p q i b", b=2),
                                     adjT[:, :, ds((i + s * Q) * P, P), :], ACT.Copy, scale=1.0 / KEEP) \
                  .then_inc(s_k16, 1)
            in_pairs(act, to16)

        @block.vector
        def _(dve):
            def variance(i, s, base, src):
                t = i * 2 + s
                if base == 0:
                    dve.wait_ge(s_x[s], loaded(i, s))
                nc.vector.bn_stats(stats[:, s, :], src(i, s)).then_inc(s_bn, 1)
                dve.wait_ge(s_bn, t + (base + 1))
                if base or not early(i):
                    dve.wait_ge(s_hn, t + (base - 1))
                nc.vector.tensor_tensor(both[:, s, :], stats[:, s, 1:3], stats[:, s, 4:6], ALU.add)
                nc.vector.tensor_tensor(gap[:, s, 0:1], stats[:, s, 1:2], stats[:, s, 4:5], ALU.subtract) \
                  .then_inc(s_gap, 1)
                dve.wait_ge(s_gap, t + (base + 1))
                nc.vector.scalar_tensor_tensor(out=gap[:, s, 1:2], in0=gap[:, s, 0:1], scalar=C / 4,
                                               in1=gap[:, s, 0:1], op0=ALU.mult, op1=ALU.mult).then_inc(s_gap2, 1)
                dve.wait_ge(s_gap2, t + (base + 1))
                nc.vector.tensor_tensor(cvar[:, s:s + 1], both[:, s, 1:2], gap[:, s, 1:2], ALU.add).then_inc(s_mv, 1)

            def coefs(i, s, base):
                t = i * 2 + s
                dve.wait_ge(s_std, t + (base + 1))
                nc.vector.reciprocal(rstd[:, s:s + 1], std[:, s:s + 1]).then_inc(s_rstd, 1)
                dve.wait_ge(s_rstd, t + (base + 1))
                nc.vector.scalar_tensor_tensor(out=nbias[:, s:s + 1], in0=both[:, s, 0:1], scalar=-0.5,
                                               in1=rstd[:, s:s + 1], op0=ALU.mult, op1=ALU.mult).then_inc(s_coef, 1)

            def copy_half(i, g, b, offset, of, to):
                dve.wait_ge(of, i * 2 + (offset + g + 1))
                nc.vector.tensor_copy(adjT16[:, HS[g]:HS[g] + HB[g], ds((i + b * Q) * P, P)],
                                      psw[:, 6 + g, 0:HB[g] * P].rearrange("p (j i) -> p j i", i=P)).then_inc(to, 1)

            def hT_low(i, s, base):
                dve.wait_ge(s_hi, i * 2 + s + (base + 1))
                nc.vector.scalar_tensor_tensor(out=hT16[:, s, 1, :], in0=ps[:, s, :], scalar=XS, in1=hT16[:, s, 0, :],
                                               op0=ALU.mult, op1=ALU.subtract).then_inc(s_lo, 1)

            def copy_h(i, s):
                dve.wait_ge(s_mm, i * 2 + s + 1)
                L = i + s * Q
                nc.vector.tensor_scalar(tile_of(slots[:, 1:H + 1], L), by_head(ps[:, 2 + s, :]), 1.0 / (XS * WS), None,
                                        ALU.mult)
                nc.vector.tensor_scalar(sn[:, :, ds(L, 1)].rearrange("p h a -> p (h a)"), ps[:, 4 + s, 0:2 * H],
                                        1.0 / (XS * WS), None, ALU.mult).then_inc(s_hev, 1)

            def x_stats_src(i, s):
                return xb[:, s, :]

            def stage_a(i, s, first, last):
                if not last:
                    coefs(*nxt(i, s), 0)
                hT_low(i, s, 0)
                if not first:
                    copy_half(*prv(i, s), 0, 0, s_g, s_gev)
                if has_nxt2(i):
                    variance(i + 1, s, 0, x_stats_src)
                if not first:
                    copy_h(*prv(i, s))

            variance(0, 0, 0, x_stats_src)
            coefs(0, 0, 0)
            variance(0, 1, 0, x_stats_src)
            dve.wait_ge(s_w0, HALVES)
            dve.wait_ge(s_av, 2 * HALVES)
            n = 0
            for a in range(2):
                for k in range(KT):
                    if n:
                        dve.wait_ge(s_wa, n)
                    nc.vector.tensor_tensor(hmean[:, :], W_raw[:, k, :], a_bc[:, a, :], ALU.mult).then_inc(s_wap, 1)
                    n += 1
                    dve.wait_ge(s_wap, n)
                    nc.vector.tensor_reduce(wa[:, k, a * H:(a + 1) * H], by_head(hmean[:, :]),
                                            AX_X, ALU.add).then_inc(s_wa, 1)
            dve.wait_ge(s_wh, 1)
            nc.vector.scalar_tensor_tensor(out=W16[:, 1, :, :], in0=W_raw, scalar=WS, in1=W16[:, 0, :, :],
                                           op0=ALU.mult, op1=ALU.subtract).then_inc(s_wl16, 1)
            dve.wait_ge(s_wa, 2 * KT)
            nc.vector.tensor_scalar(wa16[:, 0, :, :], wa[:, :, :], WS, None, ALU.mult).then_inc(s_wl16, 1)
            dve.wait_ge(s_wl16, 2)
            nc.vector.scalar_tensor_tensor(out=wa16[:, 1, :, :], in0=wa[:, :, :], scalar=WS, in1=wa16[:, 0, :, :],
                                           op0=ALU.mult, op1=ALU.subtract).then_inc(s_wl16, 2)
            in_pairs(dve, stage_a, peel=2)
            copy_half(Q - 1, 1, 0, 0, s_g, s_gev)
            copy_h(Q - 1, 1)

            dve.wait_ge(s_hev, NT)
            nc.vector.tensor_reduce(top[:, 0:H], sn[:, H:2 * H, :], AX_X, ALU.max).then_inc(s_top, 1)
            dve.wait_ge(s_topa, 1)
            tops = topa[:, 0:H].unsqueeze(2).to_broadcast([P, H, NT])
            nc.vector.tensor_tensor(r_i[:, :, :], sn[:, 0:H, :], tops, ALU.add).then_inc(s_nd1, 1)
            dve.wait_ge(s_nd1, 1)
            nc.vector.tensor_scalar(r_i[:, :, :], r_i[:, :, :], U_TOP, None, ALU.min).then_inc(s_nd, 1)
            nc.vector.tensor_tensor(Fj[:, :, :], sn[:, H:2 * H, :], tops, ALU.subtract).then_inc(s_nd, 1)
            dve.wait_ge(s_hsh, 1)
            nc.vector.scalar_tensor_tensor(out=hsum16[:, 1, :, :], in0=ps[:, 1, :].rearrange("p (k n) -> p k n", k=KT),
                                           scalar=XS / N, in1=hsum16[:, 0, :, :], op0=ALU.mult, op1=ALU.subtract) \
              .then_inc(s_hsl, 1)
            dve.wait_ge(s_exp, 2)
            dve.wait_ge(s_rt, 1)
            nc.vector.tensor_scalar(nKj[:, :, :], Kj[:, :, :], -1.0, None, ALU.mult).then_inc(s_nk, 1)

            def p_step(h, c, i, s, first=False):
                step = h * (2 * NT) + i * 2 + (c * NT + s)
                dve.wait_ge(s_q, step + 1)
                if not first:
                    dve.wait_ge(s_pe, step - 1)
                nc.vector.scalar_tensor_tensor(out=Pt[:, s, :], in0=q[:, s, :],
                                               scalar=Kj[:, ds(h, 1), ds(i + s * Q, 1)].rearrange("p a b -> p (a b)"),
                                               in1=adjT[:, ds(i, 1), c * CW:(c + 1) * CW, s].rearrange("p a n -> p (a n)"),
                                               op0=ALU.add, op1=ALU.mult).then_inc(s_p, 1)

            def counts():
                dve.wait_ge(s_cast, UNITS)
                nc.vector.tensor_tensor(rcnt[:, :], cnt2[:, :, 0], cnt2[:, :, 1], ALU.add).then_inc(s_cn, 1)
                dve.wait_ge(s_cn, 1)
                nc.vector.tensor_scalar(empty[:, :], rcnt[:, :], 0.0, None, ALU.is_equal).then_inc(s_cn, 1)
                nc.vector.tensor_scalar(some[:, :], rcnt[:, :], 0.0, None, ALU.is_gt).then_inc(s_cn, 1)
                nc.vector.tensor_reduce(top[:, H:H + 1], rcnt[:, :], AX_X, ALU.max).then_inc(s_ctop, 1)
                dve.wait_ge(s_ctop, 1)
                dve.wait_ge(s_cn, 3)
                nc.vector.tensor_scalar(rcnt[:, :], rcnt[:, :], float(EDGE), float(EDGE * NEIGH), ALU.max, ALU.min) \
                  .then_inc(s_cn, 1)
                dve.wait_ge(s_cn, 4)
                nc.vector.reciprocal(rcnt[:, :], rcnt[:, :]).then_inc(s_cn, 1)
                dve.wait_ge(s_cn, 5)
                nc.vector.tensor_scalar(rcnt[:, :], rcnt[:, :], KEEP / YS, None, ALU.mult).then_inc(s_cn, 1)

            def denominators(h, c):
                rnd = h * 2 + c
                FULL = OWN * TPB
                dve.wait_ge(s_pe, (rnd + 1) * NT)
                first_bank = BANKS[c][0]
                dens = ps[:, first_bank:first_bank + OWN, 0:TPB * FA] \
                    .rearrange("p b (m f) -> p b m f", f=FA)[:, :, :, FH:FA]
                nc.vector.tensor_tensor(den[:, 0:FULL].rearrange("p (b m a) -> p b m a", m=TPB, a=1), dens,
                                        empty[:, c * Q:c * Q + FULL].rearrange("p (b m a) -> p b m a", m=TPB, a=1),
                                        ALU.add).then_inc(s_den, 1)
                for m0, m1 in ((FULL, FULL + TPB), (FULL + TPB, Q)):
                    bank = BANKS[c][m0 // TPB]
                    dens = ps[:, bank, 0:(m1 - m0) * FA].rearrange("p (m f) -> p m f", f=FA)[:, :, FH:FA]
                    nc.vector.tensor_tensor(den[:, m0:m1].rearrange("p (m a) -> p m a", a=1), dens,
                                            empty[:, c * Q + m0:c * Q + m1].rearrange("p (m a) -> p m a", a=1),
                                            ALU.add).then_inc(s_den, 1)
                dve.wait_ge(s_den, (rnd + 1) * 3)
                nc.vector.reciprocal(den[:, 0:Q], den[:, 0:Q]).then_inc(s_rden, 1)
                dve.wait_ge(s_rden, rnd + 1)

            def normalise(h, c, b):
                for m in range(b * TPB, min(b * TPB + TPB, Q)):
                    ins = nc.vector.tensor_scalar(
                        slots[:, ds(h, 1), c * Q + m, 0:FH].rearrange("p a f -> p (a f)"),
                        acc(c, m)[:, 0:FH], den[:, m:m + 1], None, ALU.mult)
                ins.then_inc(s_ev, 1)

            def round_(h, c, before, with_adj=False):
                p_step(h, c, 0, 0, first=with_adj)
                if before is not None:
                    denominators(*before)
                    for b in range(OWN, NB):
                        normalise(*before, b)
                p_step(h, c, 0, 1, first=with_adj)
                if with_adj:
                    copy_half(0, 0, 1, UNITS_A, s_g, s_gev)
                if before is not None:
                    normalise(*before, 0)
                for s in range(2):
                    p_step(h, c, 1, s)
                    if with_adj:
                        copy_half(*prv(1, s), 1, UNITS_A, s_g, s_gev)
                    if before is not None:
                        normalise(*before, 1 + s)
                with dve.Fori(2, Q) as i:
                    for s in range(2):
                        p_step(h, c, i, s)
                        if with_adj:
                            copy_half(*prv(i, s), 1, UNITS_A, s_g, s_gev)
                if with_adj:
                    copy_half(Q - 1, 1, 1, UNITS_A, s_g, s_gev)
                    counts()
                    dve.wait_ge(s_gev, UNITS)
                    dve.wait_ge(s_cn, 6)

            dve.wait_ge(s_hmc, 1)
            dve.wait_ge(s_gev, UNITS_A)
            round_(0, 0, None, with_adj=True)
            round_(0, 1, (0, 0))
            dve.wait_ge(s_ctopa, 1)
            nc.vector.tensor_scalar(flag[:, :], topa[:, H:H + 1], float(EDGE * NEIGH), None, ALU.is_gt) \
              .then_inc(s_flag, 1)
            with dve.Fori(1, H) as h:
                round_(h, 0, (h - 1, 1))
                round_(h, 1, (h, 0))
            denominators(H - 1, 1)
            for b in range(NB):
                normalise(H - 1, 1, b)

            dve.wait_ge(s_flag, 1)
            many = dve.value_load(flag[0:1, 0:1], min_val=0, max_val=1)
            with dve.If(many > 0):
                nc.vector.memset(c_keep8[:, N:NP], 0).then_inc(c_zero, 1)
                nc.vector.memset(count[:, 0:1], 0).then_inc(c_zero, 1)
                dve.wait_ge(c_zero, 2)

                def c1(i, b, first, last):
                    t = i * 2 + b
                    dve.wait_ge(c_adjs, HALVES * (NT - 1 + NR) if last else i * (2 * HALVES) + (b + 1) * HALVES)
                    if not first:
                        dve.wait_ge(c_keep, t)
                    nc.vector.tensor_tensor_scan(count[:, 1:N + 1], c_adj[:, 0:N], cap[:, 0:1].to_broadcast([P, N]),
                                                 0.0, ALU.add, ALU.min).then_inc(c_scan, 1)
                    dve.wait_ge(c_scan, t + 1)
                    if not first:
                        dve.wait_ge(c_g, t * 2)
                    nc.vector.tensor_tensor(c_keep8[:, 0:N], count[:, 1:N + 1], count[:, 0:N],
                                            ALU.subtract).then_inc(c_dif, 1)
                    dve.wait_ge(c_dif, t + 1)
                    nc.vector.tensor_scalar(c_keep8[:, 0:N], c_keep8[:, 0:N], float(EDGE), None,
                                            ALU.mult).then_inc(c_keep, 1)
                    for g in range(2):
                        dve.wait_ge(c_g, t * 2 + g + 1)
                        nc.vector.tensor_copy(adjT16[:, HS[g]:HS[g] + HB[g], ds((i + b * Q) * P, P)],
                                              psw[:, 6 + g, 0:HB[g] * P].rearrange("p (j i) -> p j i", i=P)) \
                          .then_inc(c_gev, 1)
                in_pairs(dve, c1)
                dve.wait_ge(c_gev, UNITS)

            for k in range(KT):
                for w in range(2):
                    dve.wait_ge(s_wtc[0], 2 * k + w + 1)
                    nc.vector.scalar_tensor_tensor(out=wT16[:, w, 1, k, :], in0=ps[:, 2 * (k % 2) + w, :], scalar=WS,
                                                   in1=wT16[:, w, 0, k, :], op0=ALU.mult, op1=ALU.subtract) \
                      .then_inc(s_wtc[1], 1)

            def x1_variance(i, s):
                dve.wait_ge(s_xo, i * 2 + s + 1)
                o = tile_of(slots, i + s * Q)
                nc.vector.scalar_tensor_tensor(out=o, in0=by_head(hmean[:, :]), scalar=empty[:, ds(i + s * Q, 1)], in1=o,
                                               op0=ALU.mult, op1=ALU.add).then_inc(s_x1, 1)
                dve.wait_ge(s_x1, i * 2 + s + 1)
                nc.vector.memset(den[:, 0:1], 0.0)
                variance(i, s, LN_A, lambda i, s: tile_of(slots, i + s * Q))

            def y_low(i, s):
                dve.wait_ge(s_yhi, i * 2 + s + 1)
                nc.vector.scalar_tensor_tensor(
                    out=y16[:, 0:H, ds(i + s * Q, 1), 1, :].rearrange("p h a f -> p h (a f)"),
                    in0=by_head(ps[:, 2 + s, :]), scalar=YS / (XS * WS),
                    in1=y16[:, 0:H, ds(i + s * Q, 1), 0, :].rearrange("p h a f -> p h (a f)"),
                    op0=ALU.mult, op1=ALU.subtract).then_inc(s_ylo, 1)

            def leaky_z(i, s):
                dve.wait_ge(s_z, i * 2 + s + 1)
                nc.vector.scalar_tensor_tensor(out=zt[:, s, :], in0=ps[:, 4 + s, :], scalar=1.0 / (XS * WS), in1=bline,
                                               op0=ALU.mult, op1=ALU.add).then_inc(s_zt, 1)
                dve.wait_ge(s_zt, i * 2 + s + 1)
                if not early(i):
                    dve.wait_ge(s_zo, i * 2 + s - 1)
                nc.vector.scalar_tensor_tensor(out=zl[:, s, :], in0=zt[:, s, :], scalar=SLOPE, in1=zt[:, s, :],
                                               op0=ALU.mult, op1=ALU.max).then_inc(s_zl, 1)

            def stage_c2(i, s, first, last):
                if has_nxt2(i):
                    x1_variance(i + 1, s)
                hT_low(i, s, LN_A)
                if not early(i):
                    y_low(i - 1, s)
                if has_nxt2(i):
                    coefs(i + 1, s, LN_A)
                if not first:
                    leaky_z(*prv(i, s))

            dve.wait_ge(s_bl, HALVES)
            x1_variance(0, 0)
            coefs(0, 0, LN_A)
            x1_variance(0, 1)
            coefs(0, 1, LN_A)
            in_pairs(dve, stage_c2, peel=2)
            leaky_z(Q - 1, 1)
            for s in range(2):
                y_low(Q - 1, s)

            dve.wait_ge(s_bnb, HALVES)

            def stage_d(i, s, first, last):
                t = i * 2 + s
                L = i + s * Q
                dve.wait_ge(s_nb, t + 1)
                nc.vector.scalar_tensor_tensor(out=dt_[:, s, :], in0=ps[:, s, :], scalar=rcnt[:, ds(L, 1)], in1=bnb,
                                               op0=ALU.mult, op1=ALU.add).then_inc(s_dt, 1)
                dve.wait_ge(s_dt, t + 1)
                nc.vector.scalar_tensor_tensor(out=dl[:, s, :], in0=dt_[:, s, :], scalar=SLOPE, in1=dt_[:, s, :],
                                               op0=ALU.mult, op1=ALU.max).then_inc(s_dl, 1)
                dve.wait_ge(s_dl, t + 1)
                dve.wait_ge(s_zin[s], i * HALVES + HALVES)
                if not early(i):
                    dve.wait_ge(s_out[s], i * HALVES)
                nc.vector.scalar_tensor_tensor(out=do[:, s, :], in0=dl[:, s, :], scalar=some[:, ds(L, 1)],
                                               in1=zin[:, s, :], op0=ALU.mult, op1=ALU.add).then_inc(s_do, 1)
            in_pairs(dve, stage_d)

        @block.tensor
        def _(pe):
            def transposes(i, s, base):
                pe.wait_ge(s_hn, i * 2 + s + (base + 1))
                if not early(i):
                    pe.wait_ge(s_lo, i * 2 + s + (base - 1))
                for k in range(KT):
                    ins = nc.tensor.transpose(ps[:, s, k * P:(k + 1) * P], hn[:, s, k * P:(k + 1) * P], ident[:, :])
                ins.then_inc(s_xT, 1)

            def half(g, src):
                for k in range(HB[g]):
                    j = HS[g] + k
                    ins = nc.tensor.transpose(psb[:, 6 + g, k * P:(k + 1) * P],
                                              src[:, j * 2 * P:(j + 1) * 2 * P].bitcast(BF16), ident_b[:, :])
                return ins

            def adj_half(i, g, b, src):
                u = i * 2 + (g + b * UNITS_A)
                pe.wait_ge(s_cast, u + 1)
                if b or not early(i):
                    pe.wait_ge(s_gev, u - 1)
                half(g, src).then_inc(s_g, 1)

            def split_product(dst, x_hi, x_lo, w_hi, w_lo, k):
                nc.tensor.matmul(dst, x_hi, w_hi, start=(k == 0), stop=False)
                nc.tensor.matmul(dst, x_hi, w_lo, start=False, stop=False)
                return nc.tensor.matmul(dst, x_lo, w_hi, start=False, stop=(k == KT - 1))

            def product(i, s):
                t = i * 2 + s
                pe.wait_ge(s_lo, t + 1)
                if not early(i):
                    pe.wait_ge(s_hev, t - 1)
                for k in range(KT):
                    x_hi, x_lo = (hT16[:, s, part, k * P:(k + 1) * P] for part in range(2))
                    split_product(ps[:, 2 + s, :], x_hi, x_lo, W16[:, 0, k, :], W16[:, 1, k, :], k)
                    ins = split_product(ps[:, 4 + s, 0:2 * H], x_hi, x_lo, wa16[:, 0, k, :], wa16[:, 1, k, :], k)
                ins.then_inc(s_mm, 1)

            def stage_a(i, s, first, last):
                transposes(i, s, 0)
                if not first:
                    adj_half(*prv(i, s), 0, adj8_a)
                    product(*prv(i, s))

            pe.wait_ge(s_const, 8)
            pe.wait_ge(s_wl16, 4)
            in_pairs(pe, stage_a, peel=2)
            adj_half(Q - 1, 1, 0, adj8_a)
            product(Q - 1, 1)

            pe.wait_ge(s_hsum, NT)
            for k in range(KT):
                ins = nc.tensor.matmul(ps[:, 1, k * P:(k + 1) * P], hsum[:, k * P:(k + 1) * P], ones[:, :],
                                       start=True, stop=True)
            ins.then_inc(s_hst, 1)
            pe.wait_ge(s_exp, 1)
            nc.tensor.transpose(ps[0:H * NT, 0, 0:P], r_i[:, :, :].rearrange("p h t -> p (h t)"), ident[:, :]) \
              .then_inc(s_rt, 1)
            pe.wait_ge(s_hsl, 1)
            pe.wait_ge(s_hev, NT)
            for k in range(KT):
                ins = split_product(ps[:, 2, :], hsum16[:, 0, k, :], hsum16[:, 1, k, :], W16[:, 0, k, :],
                                    W16[:, 1, k, :], k)
            ins.then_inc(s_hm, 1)
            pe.wait_ge(s_hmc, 1)

            def step(h, c, i, s):
                fst, lst = early(i) and s == 0, is_last(i, s)
                pe.wait_ge(s_p, h * (2 * NT) + i * 2 + (c * NT + s + 1))
                for m in range(Q):
                    if fst and m == OWN * TPB and not (early(h) and c == 0):
                        pe.wait_ge(s_ev, h * (2 * NB) + ((c - 1) * NB + NB - OWN))
                    ins = nc.tensor.matmul(acc(c, m), Pt[:, s, m * P:(m + 1) * P],
                                           slots[:, ds(h + 1, 1), ds(i + s * Q, 1), :].rearrange("p a b f -> p (a b f)"),
                                           start=(fst and m % TPB == 0), stop=lst, skip_group_check=True)
                ins.then_inc(s_pe, 1)

            def round_(h, c, with_adj=False):
                if not early(h):
                    pe.wait_ge(s_ev, h * (2 * NB) + (c - 1) * NB)

                def both_steps(i, s, first, last):
                    if with_adj:
                        adj_half(i, s, 1, adj8_b)
                    step(h, c, i, s)
                in_pairs(pe, both_steps)

            round_(0, 0, with_adj=True)
            pe.wait_ge(s_gev, UNITS)
            round_(0, 1)
            with pe.Fori(1, H) as h:
                for c in range(2):
                    round_(h, c)
            pe.wait_ge(s_ev, H * 2 * NB)

            pe.wait_ge(s_flag, 1)
            many = pe.value_load(flag[0:1, 0:1], min_val=0, max_val=1)
            with pe.If(many > 0):
                def c1(i, b, first, last):
                    t = i * 2 + b
                    for g in range(2):
                        if not first:
                            pe.wait_ge(c_gev, t * 2 + g - 1)
                        pe.wait_ge(c_keep, t + 1)
                        half(g, c_keep8).then_inc(c_g, 1)
                in_pairs(pe, c1)
                pe.wait_ge(c_gev, UNITS)

            pe.wait_ge(s_wnb, HALVES)
            pe.wait_ge(s_wl, HALVES)
            for k in range(KT):
                for w, raw in enumerate((w_nb_raw, w_line_raw)):
                    if k >= 2:
                        pe.wait_ge(s_wtc[1], 2 * (k - 2) + w + 1)
                    for o in range(KT):
                        ins = nc.tensor.transpose(ps[:, 2 * (k % 2) + w, o * P:(o + 1) * P],
                                                  raw[:, o, k * P:(k + 1) * P], ident[:, :])
                    ins.then_inc(s_wt, 1)

            def products(i, s):
                t = i * 2 + s
                pe.wait_ge(s_lo, t + (LN_A + 1))
                if not early(i):
                    pe.wait_ge(s_zt, t - 1)
                for w in (1, 0):
                    if w == 0 and not early(i):
                        pe.wait_ge(s_ylo, t - 1)
                    for k in range(KT):
                        ins = split_product(ps[:, 2 + 2 * w + s, :], hT16[:, s, 0, k * P:(k + 1) * P],
                                            hT16[:, s, 1, k * P:(k + 1) * P], wT16[:, w, 0, k, :], wT16[:, w, 1, k, :], k)
                    ins.then_inc(s_z if w else s_yz, 1)

            def stage_c2(i, s, first, last):
                transposes(i, s, LN_A)
                if not first:
                    products(*prv(i, s))

            pe.wait_ge(s_wtc[1], 2 * KT)
            in_pairs(pe, stage_c2, peel=2)
            products(Q - 1, 1)

            pe.wait_ge(s_ylo, NT)

            def stage_d(i, s, first, last):
                pe.wait_ge(s_k16, i * 2 + s + 1)
                if not early(i):
                    pe.wait_ge(s_dt, i * 2 + s - 1)
                for j in range(NT):
                    for part in range(2):
                        ins = nc.tensor.matmul(ps[:, s, :], keep16[:, s, j, :], y16[:, 0:H, j // 2 + j % 2 * Q, part, :],
                                               start=(j == 0 and part == 0), stop=(j == NT - 1 and part == 1))
                ins.then_inc(s_nb, 1)
            in_pairs(pe, stage_d)


_INS = ['x', 'adj', 'L0_gnn_W', 'L0_gnn_a_self', 'L0_gnn_a_neighs', 'L1_gnn_W_nb', 'L1_gnn_b_nb', 'L1_gnn_W_line',
        'L1_gnn_b_line']


def kernel(**inputs):
    import numpy as _np
    import concourse.bacc as _bacc
    from concourse import mybir as _mybir
    from concourse.bass_utils import run_bass_kernel_spmd as _run

    nc = _bacc.Bacc("TRN2", target_bir_lowering=False, num_devices=1)
    arrays, args = {}, []
    for name in _INS:
        a = _np.ascontiguousarray(inputs[name])
        arrays[f"in_{name}_dram"] = a
        args.append(nc.dram_tensor(f"in_{name}_dram", a.shape, _mybir.dt.from_np(a.dtype), kind="ExternalInput").ap())
    args.append(nc.dram_tensor("out_0_dram", inputs['x'].shape, _mybir.dt.float32, kind="ExternalOutput").ap())
    gnn_two_layers(nc, *args)
    r = _run(nc, [arrays], core_ids=[0])
    return r.results[0]["out_0_dram"]
```

```python
from contextlib import ExitStack

import concourse.bass as bass
from concourse import mybir

F32 = mybir.dt.float32
F16 = mybir.dt.float16
BF16 = mybir.dt.bfloat16
I32 = mybir.dt.int32
U16 = mybir.dt.uint16
U8 = mybir.dt.uint8
ALU = mybir.AluOpType
ACT = mybir.ActivationFunctionType
AX_X = mybir.AxisListType.X
ds = bass.ds


def gnn_two_layers(nc, x, adj, W, a_self, a_neighs, W_nb, b_nb, W_line, b_line, out):
    N, C = x.shape
    P = 128
    Q = -(-N // (2 * P))
    NT = 2 * Q
    NP = NT * P
    LAST = N // 2 - (Q - 1) * P
    KT = C // P
    H, FH = a_self.shape[1], a_self.shape[2]
    FA = FH + 1
    CW = Q * P
    NEIGH = 64
    ALPHA = 0.2
    SLOPE = 0.01
    EPS = 1e-5
    EDGE = 192
    KEEP = 64.0
    XS = 2048.0
    WS = 256.0
    YS = 128.0
    U_TOP = 100.0
    HALVES = 16
    HB = [7, 6]
    HS = [0, HB[0]]
    HC = [(0, HB[0] * 2 * P), (HB[0] * 2 * P, N)]
    UNITS_A = NT
    UNITS = 2 * NT
    assert sum(HB) == Q and H * FH == C == 512 and N % 2 == 1
    ROWS = [(0, LAST // 16 * 16), (LAST // 16 * 16, LAST)]
    NR = len(ROWS)

    r_dram = nc.dram_tensor("r_rows", [H * NT, P], F32, kind="Internal").ap()
    r_flat = r_dram.rearrange("(a t) p -> a (t p)", a=1)
    z_dram = nc.dram_tensor("z_rows", [NP, C], F32, kind="Internal").ap()

    def node_rows(m, i, s, c0, c1, a=0, b=P):
        if isinstance(i, int):
            first = 2 * P * i + s + 2 * a
            return m[first:first + 2 * (b - a) - 1:2, c0:c1]
        rows = m[s:s + 2 * P * (Q - s) - 1:2, c0:c1].rearrange("(q m) c -> q m c", m=P)
        return rows[ds(i, 1)].rearrange("q m c -> (q m) c")

    def nxt(i, s):
        return (i, 1) if s == 0 else (i + 1, 0)

    def prv(i, s):
        return (i, 0) if s == 1 else (i - 1, 1)

    def has_nxt2(i):
        return not (isinstance(i, int) and i == Q - 1)

    with ExitStack() as ctx:
        def sb(name, shape, dt):
            return ctx.enter_context(nc.sbuf_tensor(name, shape, dt))

        def sem(name):
            return ctx.enter_context(nc.semaphore(name))

        adjT = sb("adjT", [P, Q, NP, 2], U8)
        adjT16 = adjT[:, :, :, :].rearrange("p q n b -> p q (n b)").bitcast(U16)
        slots = sb("slots", [P, H + 1, NT, FA], F32)
        flat_slots = slots[:, :, :, :].rearrange("p s t f -> p s (t f)")
        work = sb("work", [P, 6 * CW], F32)
        aux = sb("aux", [P, 6 * C], F32)

        def view(region, at, *shape, dt=F32):
            per = {F32: 1, I32: 1, F16: 2, U8: 4, BF16: 2}[dt]
            n = 1
            for k in shape:
                n *= k
            v = region[:, at:at + -(-n // per)].bitcast(dt)[:, 0:n]
            names = "abcd"[:len(shape)]
            return v.rearrange(f"p ({' '.join(names)}) -> p {' '.join(names)}", **dict(zip(names, shape)))

        adj_i = view(flat_slots[:, 0, :], 0, NP, dt=I32)
        W_raw = view(work, 0, KT, C)
        a_raw = work[0:2 * H, KT * C:KT * C + P]
        wT_a = view(flat_slots[:, H - 1, :], 0, H, C)
        r_T = aux[0:H * NT, NP // 4:NP // 4 + P]
        hsum16 = view(work, 3 * CW, 2, KT, P, dt=F16)
        adj8_a = view(work, 4 * CW - NP // 4, NP, dt=U8)
        W16 = view(work, 4 * CW, 2, KT, C, dt=F16)
        hsum = view(work, 4 * CW + KT * C, C)
        R = view(work, 0, 2, CW)
        q = view(work, 2 * CW, 2, CW)
        Pt = view(work, 4 * CW, 2, CW)
        adj8_b = view(aux, 0, NP, dt=U8)
        w_nb_raw = view(aux, 2 * C, KT, C)
        w_line_raw = [view(aux, 0, KT, C // 2), view(work, 0, KT, C // 2)]
        w_nb16 = view(aux, 2 * C, KT * KT, 2, P, dt=F16)
        w_line16 = [view(aux, 0, KT * KT // 2, 2, P, dt=F16), view(work, 0, KT * KT // 2, 2, P, dt=F16)]

        def w_raw(w, k, o):
            if w == 0:
                return w_nb_raw[:, o, k * P:(k + 1) * P]
            return w_line_raw[k // 2][:, o, k % 2 * P:(k % 2 + 1) * P]

        def w_part(w, part, k):
            if w == 0:
                return w_nb16[:, k:KT * KT:KT, part, :]
            return w_line16[k // 2][:, k % 2:KT * KT // 2:2, part, :]

        c_adj = view(work, 2 * CW, NP, dt=I32)
        c_keep8 = view(work, 2 * CW + NP, NP, dt=U8)
        count = view(flat_slots[:, H, :], 0, NP + 4, dt=U8)
        x_c2 = [view(work, 2 * C, C), view(work, CW, C)]
        bline = view(work, CW + C, C)
        hn_c2 = view(work, 2 * CW, 2, C)
        hT16_c2 = view(work, 2 * CW + 2 * C, 2, 2, C, dt=F16)
        zt, zl, zo = (view(work, 4 * CW + 2 * C * k, 2, C) for k in range(3))
        T_BANK, Y_BANK, Z_BANK = (2, 5), (3, 7), (4, 6)
        xb = view(aux, 0, 2, C)
        hn_a = view(aux, 2 * C, 2, C)
        hT16_a = view(aux, 4 * C, 2, 2, C, dt=F16)
        keep16 = view(work, 0, 2, NT, P, dt=F16)
        zin, dt_, dl, do = (view(work, NP + 2 * C * k, 2, C) for k in range(4))
        bnb = view(work, NP + 8 * C, C)
        y16 = slots[:, :, :, 0:FH].bitcast(F16).rearrange("p s t (a f) -> p s t a f", a=2)

        hmean = sb("hmean", [P, C], F32)
        aT = sb("aT", [P, 2 * H], F32)
        wa16 = sb("wa16", [P, 2, KT, 2 * H], F16)
        ident = sb("ident", [P, P], F32)
        ident_b = sb("ident_b", [P, P], BF16)
        ones = sb("ones", [P, P], F32)
        eps = sb("eps", [P, 1], F32)
        cap = sb("cap", [P, 1], F32)
        stats = sb("stats", [P, 2, 6], F32)
        both = sb("both", [P, 2, 2], F32)
        gap = sb("gap", [P, 2, 2], F32)
        cvar = sb("cvar", [P, 2], F32)
        std = sb("std", [P, 2], F32)
        rstd = sb("rstd", [P, 2], F32)
        nbias = sb("nbias", [P, 2], F32)
        sn = sb("sn", [P, 2 * H, NT], F32)
        cnt2 = sb("cnt2", [P, NT, 2], F32)
        rcnt = sb("rcnt", [P, NT], F32)
        top = sb("top", [P, H + 1], F32)
        topa = sb("topa", [P, H + 1], F32)
        Fj = sb("Fj", [P, H, NT], F32)
        r_i = sb("r_i", [P, H, NT], F32)
        Kj = sb("Kj", [P, H, NT], F32)
        nKj = r_i
        flag = sb("flag", [P, 1], I32)
        empty = sb("empty", [P, NT], F32)
        some = sb("some", [P, NT], F32)
        den = sb("den", [P, Q], F32)
        spare = sb("spare", [P, 1], F32)
        spare_a = sb("spare_a", [P, 3], F32)
        ps = ctx.enter_context(nc.psum_tensor("ps", [P, 8, C], F32))
        psb = ps[:, :, :].bitcast(BF16)
        psw = ps[:, :, :].bitcast(U16)
        TPB = 3
        NB = -(-Q // TPB)
        SHARED = NB - 3
        NRB = -(-CW // C)

        BANKS = [[2, 3, 4, 0, 1], [5, 6, 7, 0, 1]]
        OWN = 3

        def acc(c, m):
            return ps[:, BANKS[c][m // TPB], (m % TPB) * FA:(m % TPB + 1) * FA]

        def tile_of(a, L):
            return a[:, 0:H, ds(L, 1), 0:FH].rearrange("p h a f -> p h (a f)")

        def by_head(v):
            return v.rearrange("p (h f) -> p h f", h=H)

        s_x = [sem(f"x_loaded{s}") for s in range(2)]
        s_adj = [sem(f"adj_half{s}_loaded") for s in range(2)]
        s_w0 = sem("w0_loaded")
        s_av = sem("a_loaded")
        s_const = sem("consts_set")
        s_xpad = sem("x_pad_row_zeroed")
        s_apad = sem("adj_pad_rows_zeroed")
        s_cpad = sem("adj8_b_pad_column_zeroed")
        s_bn = sem("bn_stats_done")
        s_gap = sem("mean_gap_done")
        s_gap2 = sem("mean_gap_squared")
        s_mv = sem("variance_done")
        s_std = sem("std_done")
        s_rstd = sem("rstd_done")
        s_coef = sem("ln_coefs_done")
        s_hn = sem("hn_done")
        s_ones = sem("ones_columns_set")
        s_hs0 = sem("hsum_zeroed")
        s_hsum = sem("hsum_added")
        s_at = sem("a_transposed")
        s_atc = sem("aT_copied")
        s_wt0 = sem("w0_transposed")
        s_wt0c = [sem("w0T_first_heads_copied"), sem("w0T_last_heads_copied")]
        s_wa = sem("wa_product_done")
        s_wh = sem("w_high_done")
        s_wl16 = sem("w_and_wa_parts_done")
        s_cast = sem("adj_half_cast")
        s_xT = sem("x_transposed")
        s_hi = sem("hT_high_done")
        s_lo = sem("hT_low_done")
        s_mm = sem("h_product_done")
        s_hev = sem("h_copied")
        s_g = sem("adj_half_transposed")
        s_gev = sem("adj_half_copied")
        s_top = sem("tops_done")
        s_topa = sem("tops_all_done")
        s_nd1 = sem("u_added")
        s_nd = sem("shifted_scores_done")
        s_exp = sem("exps_done")
        s_nk = sem("minus_k_done")
        s_rb = sem("r_rows_broadcast")
        s_rbc = sem("r_rows_copied")
        s_rt = sem("r_transposed")
        s_rtc = sem("rT_copied")
        s_rout = sem("r_stored")
        s_R = [sem(f"R_loaded{c}") for c in range(2)]
        s_cn = sem("count_steps_done")
        s_ctop = sem("count_top_done")
        s_ctopa = sem("count_top_all_done")
        s_flag = sem("flag_done")
        s_hst = sem("hsum_transposed")
        s_hsh = sem("hsum_high_done")
        s_hsl = sem("hsum_low_done")
        s_hm = sem("hmean_product_done")
        s_hmc = sem("hmean_done")
        s_q = sem("q_ready")
        s_p = sem("p_ready")
        s_pe = sem("p_consumed")
        s_den = sem("den_done")
        s_rden = sem("rden_done")
        s_ev = sem("own_bank_copied")
        s_evs = sem("shared_bank_copied")
        c_adjs = sem("c1_adj_loaded")
        c_pad = sem("c1_pad_zeroed")
        c_zero = sem("c1_zeros_set")
        c_scan = sem("c1_scan_done")
        c_dif = sem("c1_difference_done")
        c_keep = sem("c1_keep_done")
        c_g = sem("c1_half_transposed")
        c_gev = sem("c1_half_copied")
        s_wnb = sem("w_nb_loaded")
        s_wl = [sem(f"w_line_half{k}_loaded") for k in range(2)]
        s_bl = sem("b_line_loaded")
        s_bnb = sem("b_nb_loaded")
        s_wt = sem("w_transposed")
        s_wtc = [sem("wT_high_done"), sem("wT_low_done")]
        s_x2 = [sem(f"x_again_loaded{s}") for s in range(2)]
        s_xo = sem("x_added")
        s_x1 = sem("x1_done")
        s_z = sem("z_product_done")
        s_yz = sem("y_product_done")
        s_yhi = sem("y_high_done")
        s_ylo = sem("y_low_done")
        s_zt = sem("z_biased")
        s_zl = sem("z_leaky")
        s_zo = sem("z_done")
        s_zs = [sem(f"z_stored{s}") for s in range(2)]
        s_k16 = sem("keep16_done")
        s_nb = sem("neighbour_sums_done")
        s_dt = sem("mean_biased")
        s_dl = sem("mean_leaky")
        s_do = sem("out_tile_done")
        s_zin = [sem(f"z_loaded{s}") for s in range(2)]
        s_out = [sem(f"out_stored{s}") for s in range(2)]

        LN_A = NT

        def ln_buffers(base, s):
            if base == 0:
                return hn_a[:, s, :], hT16_a[:, s, :, :], ps[:, s, :]
            return hn_c2[:, s, :], hT16_c2[:, s, :, :], ps[:, T_BANK[s], :]

        LATE = Q - 4
        W_ROWS = [(0, k) for k in range(KT)] + [(1, k) for k in range(KT)]

        def w_row_at(c, t):
            g = t - 2 * LATE + (KT + 2) * c
            return g if 0 <= t - 2 * LATE and g < (KT + 2 if c == 0 else 2 * KT) else None

        def w_bank(g):
            return 5 + g % 3 if g < KT + 2 else 2 + g - (KT + 2)
        STEPS = H * 2 * NT

        def in_pairs(eng, body, stop=Q, peel=1):
            end = stop - peel if stop == Q else stop
            for i in range(peel):
                for s in range(2):
                    body(i, s, i == 0 and s == 0, False)
            with eng.Fori(peel, end) as i:
                for s in range(2):
                    body(i, s, False, False)
            for i in range(end, stop):
                for s in range(2):
                    body(i, s, False, i == Q - 1 and s == 1)

        def early(i):
            return isinstance(i, int) and i == 0

        def is_last(i, s):
            return isinstance(i, int) and i == Q - 1 and s == 1

        def loaded(i, s):
            return HALVES * (Q - 1 + NR) if is_last(i, s) else i * HALVES + HALVES

        block = ctx.enter_context(nc.Block())

        @block.sync
        def _(sp):
            def load_x(i, s, semaphore):
                for a, b in ROWS if is_last(i, s) else [(0, P)]:
                    dst = xb[a:b, s, :] if semaphore is s_x else x_c2[s][a:b, :]
                    sp.dma_start(dst, node_rows(x, i, s, 0, C, a, b)).then_inc(semaphore[s], HALVES)

            def load_adj(i, b, g):
                c0, c1 = HC[g]
                for r0, r1 in ROWS if is_last(i, b) else [(0, P)]:
                    sp.dma_start(adj_i[r0:r1, c0:c1], node_rows(adj, i, b, c0, c1, r0, r1)) \
                      .then_inc(s_adj[g], HALVES)

            def stage_a(i, s, first, last):
                if not last:
                    ni, ns = nxt(i, s)
                    if not first:
                        sp.wait_ge(s_hn, i * 2 + s)
                    if is_last(ni, ns):
                        sp.wait_ge(s_xpad, 1)
                    load_x(ni, ns, s_x)
                if not early(i):
                    sp.wait_ge(s_cast, i * 2 + s - 1)
                load_adj(i, 0, s)

            load_x(0, 0, s_x)
            sp.dma_start(W_raw, W.rearrange("(k p) n -> p k n", p=P)).then_inc(s_w0, HALVES)
            for k, a in enumerate((a_self, a_neighs)):
                sp.dma_start(a_raw[k * H:(k + 1) * H, :], a.rearrange("a h f -> (a h) f")).then_inc(s_av, HALVES)
            in_pairs(sp, stage_a, peel=2)

            def load_r(h, c):
                sp.dma_start(R[:, c, :], r_flat[:, ds(h * NP + c * CW, CW)].to_broadcast([P, CW])) \
                  .then_inc(s_R[c], HALVES)

            def stage_b_adj(i, g):
                sp.wait_ge(s_cast, i * 2 + UNITS_A + g - 1)
                if is_last(i, 1):
                    sp.wait_ge(s_apad, g + 1)
                load_adj(i, 1, g)

            for g in range(2):
                stage_b_adj(0, g)
            sp.wait_ge(s_rtc, 1)
            sp.dma_start(r_dram, r_T).then_inc(s_rout, HALVES)
            with sp.Fori(1, Q - 1) as i:
                for g in range(2):
                    stage_b_adj(i, g)
            for g in range(2):
                stage_b_adj(Q - 1, g)
            sp.wait_ge(s_rout, HALVES)
            load_r(0, 1)
            sp.dma_start(w_nb_raw, W_nb.rearrange("(k p) n -> p k n", p=P)).then_inc(s_wnb, HALVES)

            def load_w_line(half):
                sp.dma_start(w_line_raw[half], W_line[:, half * (C // 2):(half + 1) * (C // 2)]
                             .rearrange("(o p) n -> p o n", p=P)).then_inc(s_wl[half], HALVES)

            sp.wait_ge(s_g, UNITS)
            load_w_line(0)
            with sp.Fori(1, H) as h:
                for c in range(2):
                    sp.wait_ge(s_q, (h * 2 + (c - 1)) * NT)
                    load_r(h, c)
            sp.wait_ge(s_q, (2 * H - 1) * NT)
            load_w_line(1)
            load_x(0, 0, s_x2)
            sp.wait_ge(s_q, 2 * H * NT)
            load_x(0, 1, s_x2)
            sp.dma_start(bline, b_line.rearrange("(a n) -> a n", a=1).to_broadcast([P, C])).then_inc(s_bl, HALVES)
            sp.wait_ge(s_p, STEPS)

            sp.wait_ge(s_flag, 1)
            many = sp.value_load(flag[0:1, 0:1], min_val=0, max_val=1)
            with sp.If(many > 0):
                def c1(i, b, first, last):
                    if not first:
                        sp.wait_ge(c_scan, i * 2 + b)
                    if last:
                        sp.wait_ge(c_pad, 1)
                    for r0, r1 in ROWS if last else [(0, P)]:
                        sp.dma_start(c_adj[r0:r1, 0:N], node_rows(adj, i, b, 0, N, r0, r1)).then_inc(c_adjs, HALVES)
                in_pairs(sp, c1)
                sp.wait_ge(c_gev, UNITS)

            def reload(i, s, first, last):
                if not early(i):
                    sp.wait_ge(s_xo, i * 2 + s - 1)
                    load_x(i, s, s_x2)

            in_pairs(sp, reload)

            sp.wait_ge(s_zt, NT)
            sp.wait_ge(s_yz, NT)
            for s in range(2):
                sp.wait_ge(s_zs[s], HALVES * Q)
            sp.dma_start(bnb, b_nb.rearrange("(a n) -> a n", a=1).to_broadcast([P, C])).then_inc(s_bnb, HALVES)

            def store_out(i, s):
                sp.wait_ge(s_do, i * 2 + s + 1)
                for a, b in ROWS if is_last(i, s) else [(0, P)]:
                    sp.dma_start(node_rows(out, i, s, 0, C, a, b), do[a:b, s, :]).then_inc(s_out[s], HALVES)

            def stage_d(i, s, first, last):
                if not early(i):
                    sp.wait_ge(s_do, i * 2 + s - 1)
                sp.dma_start(zin[:, s, :], z_dram[ds((i + s * Q) * P, P), :]).then_inc(s_zin[s], HALVES)
                if not first:
                    store_out(*prv(i, s))

            in_pairs(sp, stage_d)
            store_out(Q - 1, 1)
            for s in range(2):
                sp.wait_ge(s_out[s], loaded(Q - 1, s))

        @block.gpsimd
        def _(pool):
            nc.gpsimd.memset(ident[:, :], 0.0).then_inc(s_const, 1)
            nc.gpsimd.memset(ones[:, :], 1.0).then_inc(s_const, 1)
            nc.gpsimd.memset(eps[:, :], EPS).then_inc(s_const, 1)
            nc.gpsimd.memset(cap[:, :], float(NEIGH)).then_inc(s_const, 1)
            nc.gpsimd.memset(adj8_a[:, N:NP], 0).then_inc(s_const, 1)
            pool.wait_ge(s_const, 5)
            nc.gpsimd.affine_select(out=ident[:, :], in_=ident[:, :], compare_op=ALU.not_equal, fill=1.0, base=0,
                                    pattern=[[-1, P]], channel_multiplier=1).then_inc(s_const, 1)
            pool.wait_ge(s_const, 6)
            nc.gpsimd.tensor_copy(ident_b[:, :], ident[:, :]).then_inc(s_const, 1)
            nc.gpsimd.memset(hsum, 0.0).then_inc(s_hs0, 1)
            pool.wait_ge(s_hs0, 1)
            pool.wait_ge(s_wa, 1)
            nc.gpsimd.memset(slots[:, 1:H + 1, :, FH:FA], 1.0).then_inc(s_ones, 1)

            def sum_h(i, s, first, last):
                pool.wait_ge(s_hn, i * 2 + s + 1)
                if not first:
                    pool.wait_ge(s_hsum, i * 2 + s)
                nc.gpsimd.tensor_tensor(hsum, hsum, hn_a[:, s, :], ALU.add).then_inc(s_hsum, 1)

            in_pairs(pool, sum_h, stop=Q - 1)
            pool.wait_ge(s_hsum, NT - 2)
            nc.gpsimd.memset(xb[P - 32:P, 1, :], 0.0).then_inc(s_xpad, 1)
            pool.wait_ge(s_xpad, 1)
            sum_h(Q - 1, 0, False, False)
            sum_h(Q - 1, 1, False, True)
            pool.wait_ge(s_hsum, NT)
            nc.gpsimd.memset(adj8_b[:, N:NP], 0).then_inc(s_cpad, 1)

            pool.wait_ge(s_top, 1)
            nc.gpsimd.partition_all_reduce(topa[:, 0:H], top[:, 0:H], P, bass.bass_isa.ReduceOp.max) \
              .then_inc(s_topa, 1)
            pool.wait_ge(s_topa, 1)
            for g, (c0, c1) in enumerate(HC):
                pool.wait_ge(s_cast, UNITS - 3 + g)
                nc.gpsimd.memset(adj_i[P - 32:P, c0:c1], 0).then_inc(s_apad, 1)
                pool.wait_ge(s_apad, g + 1)
            pool.wait_ge(s_ctop, 1)
            nc.gpsimd.partition_all_reduce(topa[:, H:H + 1], top[:, H:H + 1], P, bass.bass_isa.ReduceOp.max) \
              .then_inc(s_ctopa, 1)

            def add_x(i, s):
                pool.wait_ge(s_x2[s], loaded(i, s))
                o = tile_of(slots, i + s * Q)
                nc.gpsimd.tensor_tensor(o, by_head(x_c2[s]), o, ALU.add).then_inc(s_xo, 1)

            pool.wait_ge(s_ev, (2 * H - 1) * OWN)
            pool.wait_ge(s_evs, (2 * H - 1) * SHARED)
            add_x(0, 0)
            pool.wait_ge(s_flag, 1)
            many = pool.value_load(flag[0:1, 0:1], min_val=0, max_val=1)
            with pool.If(many > 0):
                pool.wait_ge(c_scan, NT - 1)
                nc.gpsimd.memset(c_adj[P - 32:P, :], 0).then_inc(c_pad, 1)
                pool.wait_ge(c_gev, UNITS)

            def add_z(i, s):
                pool.wait_ge(s_zl, i * 2 + s + 1)
                if not early(i):
                    pool.wait_ge(s_zs[s], i * HALVES)
                nc.gpsimd.tensor_tensor(by_head(zo[:, s, :]), by_head(zl[:, s, :]), tile_of(slots, i + s * Q),
                                        ALU.add).then_inc(s_zo, 1)

            def stage_c2(i, s, first, last):
                if has_nxt2(i) and not is_last(*nxt(i, s)) and not (isinstance(i, int) and i == Q - 2 and s == 1):
                    add_x(*nxt(i + 1, s))
                if not first:
                    add_z(*prv(i, s))

            pool.wait_ge(s_ev, (2 * H - 1) * OWN + 1)
            add_x(0, 1)
            add_x(1, 0)
            pool.wait_ge(s_ev, 2 * H * OWN)
            pool.wait_ge(s_evs, 2 * H * SHARED)
            in_pairs(pool, stage_c2, peel=2)
            add_z(Q - 1, 1)

        @block.scalar
        def _(act):
            def std_(i, s, base):
                act.wait_ge(s_mv, i * 2 + s + (base + 1))
                nc.scalar.activation(std[:, s:s + 1], cvar[:, s:s + 1], ACT.Sqrt, bias=eps[:, 0:1],
                                     scale=1.0 / C).then_inc(s_std, 1)

            def relu(i, s, base, src, semaphores):
                t = i * 2 + s
                act.wait_ge(s_coef, t + (base + 1))
                if not early(i):
                    for sm, v in semaphores:
                        act.wait_ge(sm, t + (v - 1))
                nc.scalar.activation(by_head(ln_buffers(base, s)[0]), src(i, s), ACT.Relu, bias=nbias[:, s:s + 1],
                                     scale=rstd[:, s:s + 1]).then_inc(s_hn, 1)

            def cast(i, g, b, dst):
                u = i * 2 + g + b * UNITS_A
                c0, c1 = HC[g]
                if is_last(i, b):
                    act.wait_ge(s_adj[g], HALVES * (2 * Q - 1 + NR))
                else:
                    act.wait_ge(s_adj[g], i * HALVES + (b * Q + 1) * HALVES)
                if b or not early(i):
                    act.wait_ge(s_g, u - 1)
                nc.scalar.activation(dst[:, c0:c1], adj_i[:, c0:c1], ACT.Copy, scale=float(EDGE),
                                     accum_out=cnt2[:, ds(i + b * Q, 1), g]).then_inc(s_cast, 1)

            def hT_high(i, s, base):
                t = i * 2 + s
                act.wait_ge(s_xT, t + (base + 1))
                if not early(i):
                    act.wait_ge(s_mm if base == 0 else s_yz, t - 1)
                _, hT16, bank = ln_buffers(base, s)
                nc.scalar.activation(hT16[:, 0, :], bank, ACT.Copy, scale=XS).then_inc(s_hi, 1)

            def x_src(i, s):
                return by_head(xb[:, s, :])

            a_used = [(s_xT, 0), (s_hsum, 0)]

            def stage_a(i, s, first, last):
                hT_high(i, s, 0)
                if not last:
                    relu(*nxt(i, s), 0, x_src, a_used)
                cast(i, s, 0, adj8_a)
                if has_nxt2(i):
                    std_(i + 1, s, 0)

            act.wait_ge(s_const, 7)
            std_(0, 0, 0)
            relu(0, 0, 0, x_src, a_used)
            act.wait_ge(s_w0, HALVES)
            nc.scalar.activation(W16[:, 0, :, :], W_raw, ACT.Copy, scale=WS).then_inc(s_wh, 1)
            for h in range(H // 2, H):
                act.wait_ge(s_wt0, h + 1)
                nc.scalar.activation(wT_a[:, h, :], ps[:, 4 + h, :], ACT.Copy).then_inc(s_wt0c[1], 1)
            std_(0, 1, 0)
            in_pairs(act, stage_a, peel=2)

            act.wait_ge(s_hst, 1)
            nc.scalar.activation(hsum16[:, 0, :, :], ps[:, 0, :].rearrange("p (k n) -> p k n", k=KT), ACT.Copy,
                                 scale=XS / N).then_inc(s_hsh, 1)
            act.wait_ge(s_nd, 2)
            nc.scalar.activation(r_i[:, :, :], r_i[:, :, :], ACT.Exp, scale=1.0 - ALPHA).then_inc(s_exp, 1)
            nc.scalar.activation(Kj[:, :, :], Fj[:, :, :], ACT.Exp, scale=ALPHA).then_inc(s_exp, 1)
            act.wait_ge(s_exp, 2)
            nc.scalar.activation(Fj[:, :, :], Fj[:, :, :], ACT.Exp).then_inc(s_exp, 1)
            act.wait_ge(s_hm, 1)
            nc.scalar.activation(hmean[:, :], ps[:, 2, :], ACT.Copy, scale=1.0 / (XS * WS)).then_inc(s_hmc, 1)
            for b in range(NRB):
                act.wait_ge(s_rb, b + 1)
                n = min(C, CW - b * C)
                nc.scalar.activation(R[:, 0, b * C:b * C + n], ps[:, 4 + b, 0:n], ACT.Copy).then_inc(s_rbc, 1)

            act.wait_ge(s_nk, 1)
            act.wait_ge(s_exp, 3)
            act.wait_ge(s_g, UNITS_A)
            act.wait_ge(s_cpad, 1)

            def carry_wait(k):
                nc.scalar.activation(spare_a[:, k:k + 1], eps[:, :], ACT.Copy)

            def q_step(h, c, i, s, first=False):
                L = i + s * Q
                if not first:
                    act.wait_ge(s_p, h * (2 * NT) + i * 2 + (c * NT + s - 1))
                    if not isinstance(h, int) and isinstance(i, int):
                        carry_wait(s)
                nc.scalar.activation(q[:, s, :], R[:, c, :], ACT.Relu,
                                     bias=nKj[:, ds(h, 1), ds(L, 1)].rearrange("p a b -> p (a b)"),
                                     scale=Fj[:, ds(h, 1), ds(L, 1)].rearrange("p a b -> p (a b)")).then_inc(s_q, 1)

            def shared_banks(h, c):
                act.wait_ge(s_rden, h * 2 + (c + 1))
                carry_wait(2)
                for b in range(OWN, NB):
                    for m in range(b * TPB, min(b * TPB + TPB, Q)):
                        ins = nc.scalar.activation(slots[:, ds(h, 1), c * Q + m, 0:FH].rearrange("p a f -> p (a f)"),
                                                   acc(c, m)[:, 0:FH], ACT.Copy, scale=den[:, m:m + 1])
                    ins.then_inc(s_evs, 1)

            def first_steps(h, c, before):
                for s in range(2):
                    q_step(h, c, 0, s)
                shared_banks(*before)

            act.wait_ge(s_rbc, NRB)
            for s in range(2):
                q_step(0, 0, 0, s, first=True)
                if s == 0:
                    act.wait_ge(s_rt, 1)
                    nc.scalar.activation(r_T, ps[0:H * NT, 1, 0:P], ACT.Copy).then_inc(s_rtc, 1)
                cast(0, s, 1, adj8_b)
            with act.Fori(1, Q - 1) as i:
                for s in range(2):
                    q_step(0, 0, i, s)
                    cast(i, s, 1, adj8_b)
            for s in range(2):
                q_step(0, 0, Q - 1, s)
                cast(Q - 1, s, 1, adj8_b)
            act.wait_ge(s_R[1], HALVES)
            first_steps(0, 1, (0, 0))
            with act.Fori(1, Q) as i:
                for s in range(2):
                    q_step(0, 1, i, s)
            with act.Fori(1, H - 1) as h:
                for c in range(2):
                    act.wait_ge(s_R[c], h * HALVES + c * HALVES)
                    first_steps(h, c, (h, 0) if c else (h - 1, 1))
                    with act.Fori(1, Q) as i:
                        for s in range(2):
                            q_step(h, c, i, s)
            for c in range(2):
                act.wait_ge(s_R[c], (H - 1 + c) * HALVES)
                first_steps(H - 1, c, (H - 1, 0) if c else (H - 2, 1))
                with act.Fori(1, LATE) as i:
                    for s in range(2):
                        q_step(H - 1, c, i, s)
                for t in range(2 * LATE, NT):
                    q_step(H - 1, c, t // 2, t % 2)
                    g = w_row_at(c, t - 2)
                    if g is not None:
                        act.wait_ge(s_wt, g + 1)
                        nc.scalar.activation(w_part(W_ROWS[g][0], 0, W_ROWS[g][1]),
                                             ps[:, w_bank(g), :].rearrange("p (o n) -> p o n", o=KT), ACT.Copy,
                                             scale=WS).then_inc(s_wtc[0], 1)
                    if c == 1 and t == NT - 2:
                        std_(0, 0, LN_A)

            act.wait_ge(s_flag, 1)
            many = act.value_load(flag[0:1, 0:1], min_val=0, max_val=1)
            with act.If(many > 0):
                act.wait_ge(c_gev, UNITS)

            def y_high(i, s):
                act.wait_ge(s_yz, i * 2 + s + 1)
                act.wait_ge(s_zo, i * 2 + s + 1)
                act.dma_start(z_dram[ds((i + s * Q) * P, P), :], zo[:, s, :]).then_inc(s_zs[s], HALVES)
                nc.scalar.activation(y16[:, 0:H, ds(i + s * Q, 1), 0, :].rearrange("p h a f -> p h (a f)"),
                                     by_head(ps[:, Y_BANK[s], :]), ACT.Copy, scale=YS / (XS * WS)).then_inc(s_yhi, 1)

            def x1_src(i, s):
                return tile_of(slots, i + s * Q)

            def stage_c2(i, s, first, last):
                if not early(i):
                    hT_high(i, s, LN_A)
                if early(i) and s == 1:
                    relu(1, 0, LN_A, x1_src, [(s_xT, LN_A)])
                if not early(i):
                    y_high(i - 1, s)
                if has_nxt2(i):
                    std_(i + 1, s, LN_A)
                if not early(i) and not last:
                    relu(*nxt(i, s), LN_A, x1_src, [(s_xT, LN_A)])

            act.wait_ge(s_p, STEPS)
            relu(0, 0, LN_A, x1_src, [(s_xT, LN_A)])
            hT_high(0, 0, LN_A)
            shared_banks(H - 1, 1)
            std_(0, 1, LN_A)
            relu(0, 1, LN_A, x1_src, [])
            hT_high(0, 1, LN_A)
            in_pairs(act, stage_c2, peel=2)
            y_high(Q - 1, 0)

            def to16(i, s, first, last):
                if not early(i):
                    act.wait_ge(s_nb, i * 2 + s - 1)
                nc.scalar.activation(keep16[:, s, :, :].rearrange("p (q b) i -> p q i b", b=2),
                                     adjT[:, :, ds((i + s * Q) * P, P), :], ACT.Copy, scale=1.0 / KEEP) \
                  .then_inc(s_k16, 1)
                if first:
                    y_high(Q - 1, 1)
                    act.wait_ge(s_zt, NT)

            act.wait_ge(s_z, NT)
            in_pairs(act, to16)

        @block.vector
        def _(dve):
            def variance(i, s, base, src):
                t = i * 2 + s
                if base == 0:
                    dve.wait_ge(s_x[s], loaded(i, s))
                nc.vector.bn_stats(stats[:, s, :], src(i, s)).then_inc(s_bn, 1)
                dve.wait_ge(s_bn, t + (base + 1))
                if base or not early(i):
                    dve.wait_ge(s_hn, t + (base - 1))
                nc.vector.tensor_tensor(both[:, s, :], stats[:, s, 1:3], stats[:, s, 4:6], ALU.add)
                nc.vector.tensor_tensor(gap[:, s, 0:1], stats[:, s, 1:2], stats[:, s, 4:5], ALU.subtract) \
                  .then_inc(s_gap, 1)
                dve.wait_ge(s_gap, t + (base + 1))
                nc.vector.scalar_tensor_tensor(out=gap[:, s, 1:2], in0=gap[:, s, 0:1], scalar=C / 4,
                                               in1=gap[:, s, 0:1], op0=ALU.mult, op1=ALU.mult).then_inc(s_gap2, 1)
                dve.wait_ge(s_gap2, t + (base + 1))
                nc.vector.tensor_tensor(cvar[:, s:s + 1], both[:, s, 1:2], gap[:, s, 1:2], ALU.add).then_inc(s_mv, 1)

            def coefs(i, s, base):
                t = i * 2 + s
                dve.wait_ge(s_std, t + (base + 1))
                nc.vector.reciprocal(rstd[:, s:s + 1], std[:, s:s + 1]).then_inc(s_rstd, 1)
                dve.wait_ge(s_rstd, t + (base + 1))
                nc.vector.scalar_tensor_tensor(out=nbias[:, s:s + 1], in0=both[:, s, 0:1], scalar=-0.5,
                                               in1=rstd[:, s:s + 1], op0=ALU.mult, op1=ALU.mult).then_inc(s_coef, 1)

            def copy_half(i, g, b, offset, of, to):
                dve.wait_ge(of, i * 2 + (offset + g + 1))
                nc.vector.tensor_copy(adjT16[:, HS[g]:HS[g] + HB[g], ds((i + b * Q) * P, P)],
                                      psw[:, 6 + g, 0:HB[g] * P].rearrange("p (j i) -> p j i", i=P)).then_inc(to, 1)

            def hT_low(i, s, base):
                dve.wait_ge(s_hi, i * 2 + s + (base + 1))
                _, hT16, bank = ln_buffers(base, s)
                nc.vector.scalar_tensor_tensor(out=hT16[:, 1, :], in0=bank, scalar=XS, in1=hT16[:, 0, :],
                                               op0=ALU.mult, op1=ALU.subtract).then_inc(s_lo, 1)

            def copy_h(i, s):
                dve.wait_ge(s_mm, i * 2 + s + 1)
                L = i + s * Q
                nc.vector.tensor_scalar(tile_of(slots[:, 1:H + 1], L), by_head(ps[:, 2 + s, :]), 1.0 / (XS * WS), None,
                                        ALU.mult)
                nc.vector.tensor_scalar(sn[:, :, ds(L, 1)].rearrange("p h a -> p (h a)"), ps[:, 4 + s, 0:2 * H],
                                        1.0 / (XS * WS), None, ALU.mult).then_inc(s_hev, 1)

            def x_stats_src(i, s):
                return xb[:, s, :]

            def stage_a(i, s, first, last):
                if not first and not last:
                    coefs(*nxt(i, s), 0)
                hT_low(i, s, 0)
                if not first:
                    copy_half(*prv(i, s), 0, 0, s_g, s_gev)
                if has_nxt2(i):
                    variance(i + 1, s, 0, x_stats_src)
                if not first:
                    copy_h(*prv(i, s))

            variance(0, 0, 0, x_stats_src)
            coefs(0, 0, 0)
            dve.wait_ge(s_at, 1)
            nc.vector.tensor_copy(aT[:, :], ps[:, 2, 0:2 * H]).then_inc(s_atc, 1)
            for h in range(H // 2):
                dve.wait_ge(s_wt0, h + 1)
                nc.vector.tensor_copy(wT_a[:, h, :], ps[:, 4 + h, :]).then_inc(s_wt0c[0], 1)
            variance(0, 1, 0, x_stats_src)
            dve.wait_ge(s_wh, 1)
            nc.vector.scalar_tensor_tensor(out=W16[:, 1, :, :], in0=W_raw, scalar=WS, in1=W16[:, 0, :, :],
                                           op0=ALU.mult, op1=ALU.subtract).then_inc(s_wl16, 1)
            coefs(0, 1, 0)
            dve.wait_ge(s_wa, 1)
            wa = ps[:, 3, 0:KT * 2 * H].rearrange("p (k n) -> p k n", k=KT)
            nc.vector.tensor_scalar(wa16[:, 0, :, :], wa, WS, None, ALU.mult).then_inc(s_wl16, 1)
            dve.wait_ge(s_wl16, 2)
            nc.vector.scalar_tensor_tensor(out=wa16[:, 1, :, :], in0=wa, scalar=WS, in1=wa16[:, 0, :, :],
                                           op0=ALU.mult, op1=ALU.subtract).then_inc(s_wl16, 2)
            in_pairs(dve, stage_a, peel=2)
            dve.wait_ge(s_hsh, 1)
            nc.vector.scalar_tensor_tensor(out=hsum16[:, 1, :, :], in0=ps[:, 0, :].rearrange("p (k n) -> p k n", k=KT),
                                           scalar=XS / N, in1=hsum16[:, 0, :, :], op0=ALU.mult, op1=ALU.subtract) \
              .then_inc(s_hsl, 1)
            copy_half(Q - 1, 1, 0, 0, s_g, s_gev)
            copy_h(Q - 1, 1)

            dve.wait_ge(s_hev, NT)
            nc.vector.tensor_reduce(top[:, 0:H], sn[:, H:2 * H, :], AX_X, ALU.max).then_inc(s_top, 1)
            dve.wait_ge(s_topa, 1)
            tops = topa[:, 0:H].unsqueeze(2).to_broadcast([P, H, NT])
            nc.vector.tensor_tensor(r_i[:, :, :], sn[:, 0:H, :], tops, ALU.add).then_inc(s_nd1, 1)
            dve.wait_ge(s_nd1, 1)
            nc.vector.tensor_scalar(r_i[:, :, :], r_i[:, :, :], U_TOP, None, ALU.min).then_inc(s_nd, 1)
            nc.vector.tensor_tensor(Fj[:, :, :], sn[:, H:2 * H, :], tops, ALU.subtract).then_inc(s_nd, 1)
            dve.wait_ge(s_exp, 2)
            dve.wait_ge(s_rt, 1)
            nc.vector.tensor_scalar(nKj[:, :, :], Kj[:, :, :], -1.0, None, ALU.mult).then_inc(s_nk, 1)

            def p_step(h, c, i, s, first=False):
                step = h * (2 * NT) + i * 2 + (c * NT + s)
                dve.wait_ge(s_q, step + 1)
                if not first:
                    dve.wait_ge(s_pe, step - 1)
                nc.vector.scalar_tensor_tensor(out=Pt[:, s, :], in0=q[:, s, :],
                                               scalar=Kj[:, ds(h, 1), ds(i + s * Q, 1)].rearrange("p a b -> p (a b)"),
                                               in1=adjT[:, ds(i, 1), c * CW:(c + 1) * CW, s].rearrange("p a n -> p (a n)"),
                                               op0=ALU.add, op1=ALU.mult).then_inc(s_p, 1)

            def counts():
                dve.wait_ge(s_cast, UNITS)
                nc.vector.tensor_tensor(rcnt[:, :], cnt2[:, :, 0], cnt2[:, :, 1], ALU.add).then_inc(s_cn, 1)
                dve.wait_ge(s_cn, 1)
                nc.vector.tensor_scalar(empty[:, :], rcnt[:, :], 0.0, None, ALU.is_equal).then_inc(s_cn, 1)
                nc.vector.tensor_scalar(some[:, :], rcnt[:, :], 0.0, None, ALU.is_gt).then_inc(s_cn, 1)
                nc.vector.tensor_reduce(top[:, H:H + 1], rcnt[:, :], AX_X, ALU.max).then_inc(s_ctop, 1)
                dve.wait_ge(s_ctop, 1)
                dve.wait_ge(s_cn, 3)
                nc.vector.tensor_scalar(rcnt[:, :], rcnt[:, :], float(EDGE), float(EDGE * NEIGH), ALU.max, ALU.min) \
                  .then_inc(s_cn, 1)
                dve.wait_ge(s_cn, 4)
                nc.vector.reciprocal(rcnt[:, :], rcnt[:, :]).then_inc(s_cn, 1)
                dve.wait_ge(s_cn, 5)
                nc.vector.tensor_scalar(rcnt[:, :], rcnt[:, :], KEEP / YS, None, ALU.mult).then_inc(s_cn, 1)

            def denominators(h, c):
                rnd = h * 2 + c
                FULL = OWN * TPB
                dve.wait_ge(s_pe, (rnd + 1) * NT)
                if c == 1 or not early(h):
                    dve.wait_ge(s_evs, rnd * SHARED)
                first_bank = BANKS[c][0]
                dens = ps[:, first_bank:first_bank + OWN, 0:TPB * FA] \
                    .rearrange("p b (m f) -> p b m f", f=FA)[:, :, :, FH:FA]
                nc.vector.tensor_tensor(den[:, 0:FULL].rearrange("p (b m a) -> p b m a", m=TPB, a=1), dens,
                                        empty[:, c * Q:c * Q + FULL].rearrange("p (b m a) -> p b m a", m=TPB, a=1),
                                        ALU.add).then_inc(s_den, 1)
                for m0, m1 in ((FULL, FULL + TPB), (FULL + TPB, Q)):
                    bank = BANKS[c][m0 // TPB]
                    dens = ps[:, bank, 0:(m1 - m0) * FA].rearrange("p (m f) -> p m f", f=FA)[:, :, FH:FA]
                    nc.vector.tensor_tensor(den[:, m0:m1].rearrange("p (m a) -> p m a", a=1), dens,
                                            empty[:, c * Q + m0:c * Q + m1].rearrange("p (m a) -> p m a", a=1),
                                            ALU.add).then_inc(s_den, 1)
                dve.wait_ge(s_den, (rnd + 1) * 3)
                nc.vector.reciprocal(den[:, 0:Q], den[:, 0:Q]).then_inc(s_rden, 1)
                dve.wait_ge(s_rden, rnd + 1)

            def normalise(h, c, b):
                for m in range(b * TPB, min(b * TPB + TPB, Q)):
                    ins = nc.vector.tensor_scalar(
                        slots[:, ds(h, 1), c * Q + m, 0:FH].rearrange("p a f -> p (a f)"),
                        acc(c, m)[:, 0:FH], den[:, m:m + 1], None, ALU.mult)
                ins.then_inc(s_ev, 1)

            def w_low(g):
                dve.wait_ge(s_wtc[0], g + 1)
                w, k = W_ROWS[g]
                nc.vector.scalar_tensor_tensor(out=w_part(w, 1, k),
                                               in0=ps[:, w_bank(g), :].rearrange("p (o n) -> p o n", o=KT), scalar=WS,
                                               in1=w_part(w, 0, k), op0=ALU.mult, op1=ALU.subtract) \
                  .then_inc(s_wtc[1], 1)

            def x1_variance(i, s):
                dve.wait_ge(s_xo, i * 2 + s + 1)
                o = tile_of(slots, i + s * Q)
                nc.vector.scalar_tensor_tensor(out=o, in0=by_head(hmean[:, :]), scalar=empty[:, ds(i + s * Q, 1)], in1=o,
                                               op0=ALU.mult, op1=ALU.add).then_inc(s_x1, 1)
                dve.wait_ge(s_x1, i * 2 + s + 1)
                nc.vector.memset(spare[:, :], 0.0)
                variance(i, s, LN_A, lambda i, s: tile_of(slots, i + s * Q))

            def last_head_round(c):
                for t in range(2 * LATE, NT):
                    p_step(H - 1, c, t // 2, t % 2)
                    g = w_row_at(c, t - 1)
                    if g is not None:
                        w_low(g)
                    if c == 1 and t == NT - 4:
                        x1_variance(0, 0)

            def round_(h, c, before, with_adj=False, until=Q):
                p_step(h, c, 0, 0, first=with_adj)
                if before is not None:
                    denominators(*before)
                p_step(h, c, 0, 1, first=with_adj)
                if with_adj:
                    copy_half(0, 0, 1, UNITS_A, s_g, s_gev)
                if before is not None:
                    normalise(*before, 0)
                for s in range(2):
                    p_step(h, c, 1, s)
                    if with_adj:
                        copy_half(*prv(1, s), 1, UNITS_A, s_g, s_gev)
                    if before is not None:
                        normalise(*before, 1 + s)
                with dve.Fori(2, until) as i:
                    for s in range(2):
                        p_step(h, c, i, s)
                        if with_adj:
                            copy_half(*prv(i, s), 1, UNITS_A, s_g, s_gev)
                if with_adj:
                    copy_half(Q - 1, 1, 1, UNITS_A, s_g, s_gev)
                    counts()
                    dve.wait_ge(s_gev, UNITS)
                    dve.wait_ge(s_cn, 6)

            dve.wait_ge(s_hmc, 1)
            dve.wait_ge(s_gev, UNITS_A)
            round_(0, 0, None, with_adj=True)
            round_(0, 1, (0, 0))
            dve.wait_ge(s_ctopa, 1)
            nc.vector.tensor_scalar(flag[:, :], topa[:, H:H + 1], float(EDGE * NEIGH), None, ALU.is_gt) \
              .then_inc(s_flag, 1)
            with dve.Fori(1, H - 1) as h:
                round_(h, 0, (h - 1, 1))
                round_(h, 1, (h, 0))
            round_(H - 1, 0, (H - 2, 1), until=LATE)
            last_head_round(0)
            round_(H - 1, 1, (H - 1, 0), until=LATE)
            last_head_round(1)
            coefs(0, 0, LN_A)

            dve.wait_ge(s_flag, 1)
            many = dve.value_load(flag[0:1, 0:1], min_val=0, max_val=1)
            with dve.If(many > 0):
                dve.wait_ge(s_pe, STEPS)
                nc.vector.memset(c_keep8[:, N:NP], 0).then_inc(c_zero, 1)
                nc.vector.memset(count[:, 0:1], 0).then_inc(c_zero, 1)
                dve.wait_ge(c_zero, 2)

                def c1(i, b, first, last):
                    t = i * 2 + b
                    dve.wait_ge(c_adjs, HALVES * (NT - 1 + NR) if last else i * (2 * HALVES) + (b + 1) * HALVES)
                    if not first:
                        dve.wait_ge(c_keep, t)
                    nc.vector.tensor_tensor_scan(count[:, 1:N + 1], c_adj[:, 0:N], cap[:, 0:1].to_broadcast([P, N]),
                                                 0.0, ALU.add, ALU.min).then_inc(c_scan, 1)
                    dve.wait_ge(c_scan, t + 1)
                    if not first:
                        dve.wait_ge(c_g, t * 2)
                    nc.vector.tensor_tensor(c_keep8[:, 0:N], count[:, 1:N + 1], count[:, 0:N],
                                            ALU.subtract).then_inc(c_dif, 1)
                    dve.wait_ge(c_dif, t + 1)
                    nc.vector.tensor_scalar(c_keep8[:, 0:N], c_keep8[:, 0:N], float(EDGE), None,
                                            ALU.mult).then_inc(c_keep, 1)
                    for g in range(2):
                        dve.wait_ge(c_g, t * 2 + g + 1)
                        nc.vector.tensor_copy(adjT16[:, HS[g]:HS[g] + HB[g], ds((i + b * Q) * P, P)],
                                              psw[:, 2 + g, 0:HB[g] * P].rearrange("p (j i) -> p j i", i=P)) \
                          .then_inc(c_gev, 1)
                in_pairs(dve, c1)
                dve.wait_ge(c_gev, UNITS)

            denominators(H - 1, 1)
            normalise(H - 1, 1, 0)
            hT_low(0, 0, LN_A)
            normalise(H - 1, 1, 1)
            normalise(H - 1, 1, 2)
            x1_variance(0, 1)
            coefs(0, 1, LN_A)

            def y_low(i, s):
                dve.wait_ge(s_yhi, i * 2 + s + 1)
                nc.vector.scalar_tensor_tensor(
                    out=y16[:, 0:H, ds(i + s * Q, 1), 1, :].rearrange("p h a f -> p h (a f)"),
                    in0=by_head(ps[:, Y_BANK[s], :]), scalar=YS / (XS * WS),
                    in1=y16[:, 0:H, ds(i + s * Q, 1), 0, :].rearrange("p h a f -> p h (a f)"),
                    op0=ALU.mult, op1=ALU.subtract).then_inc(s_ylo, 1)

            def leaky_z(i, s):
                dve.wait_ge(s_z, i * 2 + s + 1)
                nc.vector.scalar_tensor_tensor(out=zt[:, s, :], in0=ps[:, Z_BANK[s], :], scalar=1.0 / (XS * WS), in1=bline,
                                               op0=ALU.mult, op1=ALU.add).then_inc(s_zt, 1)
                dve.wait_ge(s_zt, i * 2 + s + 1)
                if not early(i):
                    dve.wait_ge(s_zo, i * 2 + s - 1)
                nc.vector.scalar_tensor_tensor(out=zl[:, s, :], in0=zt[:, s, :], scalar=SLOPE, in1=zt[:, s, :],
                                               op0=ALU.mult, op1=ALU.max).then_inc(s_zl, 1)

            def stage_c2(i, s, first, last):
                if early(i) and s == 1:
                    hT_low(0, 1, LN_A)
                if has_nxt2(i):
                    x1_variance(i + 1, s)
                if not early(i):
                    hT_low(i, s, LN_A)
                if not early(i):
                    y_low(i - 1, s)
                if has_nxt2(i):
                    coefs(i + 1, s, LN_A)
                if not first:
                    leaky_z(*prv(i, s))

            dve.wait_ge(s_bl, HALVES)
            in_pairs(dve, stage_c2, peel=2)
            leaky_z(Q - 1, 1)
            for s in range(2):
                y_low(Q - 1, s)

            dve.wait_ge(s_bnb, HALVES)

            def stage_d(i, s, first, last):
                t = i * 2 + s
                L = i + s * Q
                dve.wait_ge(s_nb, t + 1)
                nc.vector.scalar_tensor_tensor(out=dt_[:, s, :], in0=ps[:, s, :], scalar=rcnt[:, ds(L, 1)], in1=bnb,
                                               op0=ALU.mult, op1=ALU.add).then_inc(s_dt, 1)
                dve.wait_ge(s_dt, t + 1)
                nc.vector.scalar_tensor_tensor(out=dl[:, s, :], in0=dt_[:, s, :], scalar=SLOPE, in1=dt_[:, s, :],
                                               op0=ALU.mult, op1=ALU.max).then_inc(s_dl, 1)
                dve.wait_ge(s_dl, t + 1)
                dve.wait_ge(s_zin[s], i * HALVES + HALVES)
                if not early(i):
                    dve.wait_ge(s_out[s], i * HALVES)
                nc.vector.scalar_tensor_tensor(out=do[:, s, :], in0=dl[:, s, :], scalar=some[:, ds(L, 1)],
                                               in1=zin[:, s, :], op0=ALU.mult, op1=ALU.add).then_inc(s_do, 1)
            in_pairs(dve, stage_d)

        @block.tensor
        def _(pe):
            def transposes(i, s, base):
                pe.wait_ge(s_hn, i * 2 + s + (base + 1))
                if not early(i):
                    pe.wait_ge(s_lo, i * 2 + s + (base - 1))
                hn, _, bank = ln_buffers(base, s)
                for k in range(KT):
                    ins = nc.tensor.transpose(bank[:, k * P:(k + 1) * P], hn[:, k * P:(k + 1) * P], ident[:, :])
                ins.then_inc(s_xT, 1)

            def half(g, src, bank=6):
                for k in range(HB[g]):
                    j = HS[g] + k
                    ins = nc.tensor.transpose(psb[:, bank + g, k * P:(k + 1) * P],
                                              src[:, j * 2 * P:(j + 1) * 2 * P].bitcast(BF16), ident_b[:, :])
                return ins

            def adj_half(i, g, b, src):
                u = i * 2 + (g + b * UNITS_A)
                pe.wait_ge(s_cast, u + 1)
                if b or not early(i):
                    pe.wait_ge(s_gev, u - 1)
                half(g, src).then_inc(s_g, 1)

            def split_product(dst, x_hi, x_lo, w_hi, w_lo, k):
                nc.tensor.matmul(dst, x_hi, w_hi, start=(k == 0), stop=False)
                nc.tensor.matmul(dst, x_hi, w_lo, start=False, stop=False)
                return nc.tensor.matmul(dst, x_lo, w_hi, start=False, stop=(k == KT - 1))

            def product(i, s):
                t = i * 2 + s
                pe.wait_ge(s_lo, t + 1)
                if not early(i):
                    pe.wait_ge(s_hev, t - 1)
                for k in range(KT):
                    x_hi, x_lo = (hT16_a[:, s, part, k * P:(k + 1) * P] for part in range(2))
                    split_product(ps[:, 2 + s, :], x_hi, x_lo, W16[:, 0, k, :], W16[:, 1, k, :], k)
                    ins = split_product(ps[:, 4 + s, 0:2 * H], x_hi, x_lo, wa16[:, 0, k, :], wa16[:, 1, k, :], k)
                ins.then_inc(s_mm, 1)

            def stage_a(i, s, first, last):
                if not first:
                    transposes(i, s, 0)
                    adj_half(*prv(i, s), 0, adj8_a)
                    if early(i):
                        pe.wait_ge(s_wl16, 4)
                    product(*prv(i, s))

            pe.wait_ge(s_const, 7)
            pe.wait_ge(s_av, 2 * HALVES)
            nc.tensor.transpose(ps[:, 2, 0:2 * H], a_raw, ident[0:2 * H, 0:2 * H]).then_inc(s_at, 1)
            pe.wait_ge(s_w0, HALVES)
            for h in range(H):
                for k in range(KT):
                    ins = nc.tensor.transpose(ps[:, 4 + h, k * P:(k + 1) * P], W_raw[:, k, h * FH:(h + 1) * FH],
                                              ident[:, :])
                ins.then_inc(s_wt0, 1)
            transposes(0, 0, 0)
            pe.wait_ge(s_atc, 1)
            for h in range(H):
                pe.wait_ge(s_wt0c[h // (H // 2)], h % (H // 2) + 1)
                for k in range(KT):
                    ins = nc.tensor.matmul(ps[:, 3, k * 2 * H + h:(k + 1) * 2 * H:H], wT_a[:, h, k * P:(k + 1) * P],
                                           aT[:, h:2 * H:H], start=True, stop=True)
            ins.then_inc(s_wa, 1)
            in_pairs(pe, stage_a, peel=2)
            pe.wait_ge(s_hsum, NT)
            pe.wait_ge(s_lo, NT - 1)
            for k in range(KT):
                ins = nc.tensor.matmul(ps[:, 0, k * P:(k + 1) * P], hsum[:, k * P:(k + 1) * P], ones[:, :],
                                       start=True, stop=True)
            ins.then_inc(s_hst, 1)
            adj_half(Q - 1, 1, 0, adj8_a)
            product(Q - 1, 1)
            pe.wait_ge(s_hsl, 1)
            pe.wait_ge(s_hev, NT - 1)
            for k in range(KT):
                ins = split_product(ps[:, 2, :], hsum16[:, 0, k, :], hsum16[:, 1, k, :], W16[:, 0, k, :],
                                    W16[:, 1, k, :], k)
            ins.then_inc(s_hm, 1)
            pe.wait_ge(s_exp, 1)
            pe.wait_ge(s_gev, UNITS_A)
            for m in range(Q):
                ins = nc.tensor.matmul(ps[:, 4 + m // KT, m % KT * P:(m % KT + 1) * P],
                                       r_i[:, 0, m:m + 1].to_broadcast([P, P]), ident[:, :], start=True, stop=True)
                if m % KT == KT - 1 or m == Q - 1:
                    ins.then_inc(s_rb, 1)
            nc.tensor.transpose(ps[0:H * NT, 1, 0:P], r_i[:, :, :].rearrange("p h t -> p (h t)"), ident[:, :]) \
              .then_inc(s_rt, 1)
            pe.wait_ge(s_ones, 1)
            pe.wait_ge(s_hmc, 1)
            pe.wait_ge(s_rbc, NRB)
            pe.wait_ge(s_rtc, 1)

            def step(h, c, i, s):
                fst, lst = early(i) and s == 0, is_last(i, s)
                pe.wait_ge(s_p, h * (2 * NT) + i * 2 + (c * NT + s + 1))
                for m in range(Q):
                    if fst and m == OWN * TPB and not (early(h) and c == 0):
                        pe.wait_ge(s_evs, h * (2 * SHARED) + c * SHARED)
                    ins = nc.tensor.matmul(acc(c, m), Pt[:, s, m * P:(m + 1) * P],
                                           slots[:, ds(h + 1, 1), ds(i + s * Q, 1), :].rearrange("p a b f -> p (a b f)"),
                                           start=(fst and m % TPB == 0), stop=lst, skip_group_check=True)
                ins.then_inc(s_pe, 1)

            def round_(h, c, with_adj=False, with_w=False):
                if not early(h):
                    pe.wait_ge(s_ev, h * (2 * OWN) + (c - 1) * OWN)

                def both_steps(i, s, first, last):
                    if with_adj:
                        adj_half(i, s, 1, adj8_b)
                    step(h, c, i, s)

                if not with_w:
                    in_pairs(pe, both_steps)
                    return
                for s in range(2):
                    step(h, c, 0, s)
                with pe.Fori(1, LATE) as i:
                    for s in range(2):
                        step(h, c, i, s)
                for t in range(2 * LATE, NT):
                    g = w_row_at(c, t)
                    if g is not None:
                        w_row(g)
                    step(h, c, t // 2, t % 2)

            def w_row(g):
                w, k = W_ROWS[g]
                if g >= 3:
                    pe.wait_ge(s_wtc[1], g - 2)
                for o in range(KT):
                    ins = nc.tensor.transpose(ps[:, w_bank(g), o * P:(o + 1) * P], w_raw(w, k, o), ident[:, :])
                ins.then_inc(s_wt, 1)

            round_(0, 0, with_adj=True)
            pe.wait_ge(s_gev, UNITS)
            round_(0, 1)
            with pe.Fori(1, H - 1) as h:
                for c in range(2):
                    round_(h, c)
            pe.wait_ge(s_wnb, HALVES)
            pe.wait_ge(s_wl[0], HALVES)
            round_(H - 1, 0, with_w=True)
            pe.wait_ge(s_wtc[1], KT + 2)
            pe.wait_ge(s_wl[1], HALVES)
            round_(H - 1, 1, with_w=True)

            pe.wait_ge(s_flag, 1)
            many = pe.value_load(flag[0:1, 0:1], min_val=0, max_val=1)
            with pe.If(many > 0):
                def c1(i, b, first, last):
                    t = i * 2 + b
                    for g in range(2):
                        if not first:
                            pe.wait_ge(c_gev, t * 2 + g - 1)
                        pe.wait_ge(c_keep, t + 1)
                        half(g, c_keep8, bank=2).then_inc(c_g, 1)
                in_pairs(pe, c1)
                pe.wait_ge(c_gev, UNITS)

            def products(i, s):
                t = i * 2 + s
                pe.wait_ge(s_lo, t + (LN_A + 1))
                if not early(i):
                    pe.wait_ge(s_zt, t - 1)
                for w in (1, 0):
                    if w == 0 and not early(i):
                        pe.wait_ge(s_ylo, t - 1)
                    for k in range(KT):
                        ins = split_product(ps[:, (Z_BANK if w else Y_BANK)[s], :], hT16_c2[:, s, 0, k * P:(k + 1) * P],
                                            hT16_c2[:, s, 1, k * P:(k + 1) * P], w_part(w, 0, k), w_part(w, 1, k), k)
                    ins.then_inc(s_z if w else s_yz, 1)

            def stage_c2(i, s, first, last):
                if early(i) and s == 1:
                    products(0, 0)
                    pe.wait_ge(s_ev, 2 * H * OWN)
                    pe.wait_ge(s_evs, 2 * H * SHARED)
                transposes(i, s, LN_A)
                if not first and not (early(i) and s == 1):
                    products(*prv(i, s))

            pe.wait_ge(s_wtc[1], 2 * KT)
            in_pairs(pe, stage_c2, peel=2)
            products(Q - 1, 1)

            def stage_d(i, s, first, last):
                pe.wait_ge(s_k16, i * 2 + s + 1)
                if not early(i):
                    pe.wait_ge(s_dt, i * 2 + s - 1)
                for j in range(NT):
                    if first and j in (0, NT - 2):
                        pe.wait_ge(s_ylo, NT - 2 if j == 0 else NT)
                    for part in range(2):
                        ins = nc.tensor.matmul(ps[:, s, :], keep16[:, s, j, :], y16[:, 0:H, j // 2 + j % 2 * Q, part, :],
                                               start=(j == 0 and part == 0), stop=(j == NT - 1 and part == 1))
                ins.then_inc(s_nb, 1)
            in_pairs(pe, stage_d)


_INS = ['x', 'adj', 'L0_gnn_W', 'L0_gnn_a_self', 'L0_gnn_a_neighs', 'L1_gnn_W_nb', 'L1_gnn_b_nb', 'L1_gnn_W_line',
        'L1_gnn_b_line']


def kernel(**inputs):
    import numpy as _np
    import concourse.bacc as _bacc
    from concourse import mybir as _mybir
    from concourse.bass_utils import run_bass_kernel_spmd as _run

    nc = _bacc.Bacc("TRN2", target_bir_lowering=False, num_devices=1)
    arrays, args = {}, []
    for name in _INS:
        a = _np.ascontiguousarray(inputs[name])
        arrays[f"in_{name}_dram"] = a
        args.append(nc.dram_tensor(f"in_{name}_dram", a.shape, _mybir.dt.from_np(a.dtype), kind="ExternalInput").ap())
    args.append(nc.dram_tensor("out_0_dram", inputs['x'].shape, _mybir.dt.float32, kind="ExternalOutput").ap())
    gnn_two_layers(nc, *args)
    r = _run(nc, [arrays], core_ids=[0])
    return r.results[0]["out_0_dram"]
```
